# Optimizing a Trainium2 kernel written in Bass

```python
import numpy as np
import jax
import jax.numpy as jnp

def _softmax(x, axis=-1):
    return jax.nn.softmax(x, axis=axis)

def _gelu(x):
    return jax.nn.gelu(x, approximate=True)

def _silu(x):
    return jax.nn.silu(x)

def _sigmoid(x):
    return jax.nn.sigmoid(x)

def _layernorm(x, axis=-1, eps=1e-05):
    m = jnp.mean(x, axis=axis, keepdims=True)
    v = jnp.var(x, axis=axis, keepdims=True)
    return (x - m) / jnp.sqrt(v + eps)

def _scatter_add(tgt, idx, src, axis=0):
    return tgt.at[idx].add(src)

def _segment_sum(src, seg, n):
    return jax.ops.segment_sum(src, seg, n)
kernel_name = 'mk_recurrent_d1_jaxref_r8_c5c083'

def setup_inputs(seed: int=0):
    np.random.seed(seed)
    _w = jnp.asarray

    def _L0_attn_setup():
        import jax, jax.numpy as jnp
        import numpy as np
        INV_SQRT2 = 0.7071067811865476

        def _haar_wavedec(x, level):
            details = []
            a = x
            for _ in range(level):
                e, o = (a[:, :, 0::2, :], a[:, :, 1::2, :])
                details.append((e - o) * INV_SQRT2)
                a = (e + o) * INV_SQRT2
            return [a] + details[::-1]

        def _haar_idwt_step(a, d):
            e = (a + d) * INV_SQRT2
            o = (a - d) * INV_SQRT2
            B, H, Lh, Dh = a.shape
            return jnp.stack([e, o], axis=3).reshape(B, H, 2 * Lh, Dh)
        key = jax.random.key(seed)
        ks = jax.random.split(key, 6)
        B, L, D, H, M = (8, 512, 128, 16, 3)
        Dh = D // H
        return {'query': jax.random.normal(ks[0], (B, L, D), jnp.float32), 'W_qkv': jax.random.normal(ks[1], (3 * D, D), jnp.float32) * 0.02, 'b_qkv': jnp.zeros((3 * D,), jnp.float32), 'W_out': jax.random.normal(ks[2], (D, D), jnp.float32) * 0.02, 'b_out': jnp.zeros((D,), jnp.float32), 'weight_q': jax.random.normal(ks[3], (H, M, Dh), jnp.float32), 'weight_v': jax.random.normal(ks[4], (H, M, Dh), jnp.float32)}
    _L0_attn_in = _L0_attn_setup()

    def _L0_ffn_setup():
        import jax, jax.numpy as jnp
        import numpy as np
        D = 128
        E = 8
        H = 256
        TOP_K = 2
        ALPHA = 0.5
        LN_EPS = 1e-05

        def _experts_all(x, W1, b1, W2, b2):
            h = jax.nn.relu(jnp.einsum('bld,edh->eblh', x, W1) + b1[:, None, None, :])
            return jnp.einsum('eblh,ehd->ebld', h, W2) + b2[:, None, None, :]

        def _selected_expert(x, expert_idx, W1, b1, W2, b2):
            oh = jax.nn.one_hot(expert_idx, E, dtype=x.dtype)
            return jnp.einsum('ebld,ble->bld', _experts_all(x, W1, b1, W2, b2), oh)

        def _layer_norm(x, gamma, beta):
            mu = jnp.mean(x, axis=-1, keepdims=True)
            var = jnp.mean(jnp.square(x - mu), axis=-1, keepdims=True)
            return (x - mu) * jax.lax.rsqrt(var + LN_EPS) * gamma + beta
        key = jax.random.key(seed)
        ks = jax.random.split(key, 8)
        x = jax.random.normal(ks[0], (2, 256, D), dtype=jnp.float32)
        gate_W = jax.random.normal(ks[1], (D, E), dtype=jnp.float32) * 0.02
        gate_b = jnp.zeros((E,), dtype=jnp.float32)
        W1 = jax.random.normal(ks[2], (E, D, H), dtype=jnp.float32) * 0.02
        b1 = jnp.zeros((E, H), dtype=jnp.float32)
        W2 = jax.random.normal(ks[3], (E, H, D), dtype=jnp.float32) * 0.02
        b2 = jnp.zeros((E, D), dtype=jnp.float32)
        ln_gamma = jnp.ones((D,), dtype=jnp.float32)
        ln_beta = jnp.zeros((D,), dtype=jnp.float32)
        return {'x': x, 'gate_W': gate_W, 'gate_b': gate_b, 'W1': W1, 'b1': b1, 'W2': W2, 'b2': b2, 'ln_gamma': ln_gamma, 'ln_beta': ln_beta}
    _L0_ffn_in = _L0_ffn_setup()
    _d = {'L0_attn_query': _L0_attn_in['query'], 'L0_attn_W_qkv': _L0_attn_in['W_qkv'], 'L0_attn_b_qkv': _L0_attn_in['b_qkv'], 'L0_attn_W_out': _L0_attn_in['W_out'], 'L0_attn_b_out': _L0_attn_in['b_out'], 'L0_attn_weight_q': _L0_attn_in['weight_q'], 'L0_attn_weight_v': _L0_attn_in['weight_v'], 'L0_ffn_gate_W': _L0_ffn_in['gate_W'], 'L0_ffn_gate_b': _L0_ffn_in['gate_b'], 'L0_ffn_W1': _L0_ffn_in['W1'], 'L0_ffn_b1': _L0_ffn_in['b1'], 'L0_ffn_W2': _L0_ffn_in['W2'], 'L0_ffn_b2': _L0_ffn_in['b2'], 'L0_ffn_ln_gamma': _L0_ffn_in['ln_gamma'], 'L0_ffn_ln_beta': _L0_ffn_in['ln_beta']}
    _x0 = _d['L0_attn_query']
    _d['L0_attn_query'] = jax.random.normal(jax.random.fold_in(jax.random.key(seed), 1), (16, 256, 128), dtype=_x0.dtype)
    del _x0
    return _d

def reference(L0_attn_query, L0_attn_W_qkv, L0_attn_b_qkv, L0_attn_W_out, L0_attn_b_out, L0_attn_weight_q, L0_attn_weight_v, L0_ffn_gate_W, L0_ffn_gate_b, L0_ffn_W1, L0_ffn_b1, L0_ffn_W2, L0_ffn_b2, L0_ffn_ln_gamma, L0_ffn_ln_beta):

    def _L0_attn_ref(query, W_qkv, b_qkv, W_out, b_out, weight_q, weight_v):
        import jax, jax.numpy as jnp
        import numpy as np
        INV_SQRT2 = 0.7071067811865476

        def _haar_wavedec(x, level):
            details = []
            a = x
            for _ in range(level):
                e, o = (a[:, :, 0::2, :], a[:, :, 1::2, :])
                details.append((e - o) * INV_SQRT2)
                a = (e + o) * INV_SQRT2
            return [a] + details[::-1]

        def _haar_idwt_step(a, d):
            e = (a + d) * INV_SQRT2
            o = (a - d) * INV_SQRT2
            B, H, Lh, Dh = a.shape
            return jnp.stack([e, o], axis=3).reshape(B, H, 2 * Lh, Dh)
        B, L, D = query.shape
        H, M, Dh = weight_q.shape
        qkv = query @ W_qkv.T + b_qkv
        q = qkv[..., :D].reshape(B, L, H, Dh).transpose(0, 2, 1, 3)
        v = qkv[..., 2 * D:].reshape(B, L, H, Dh).transpose(0, 2, 1, 3)
        cq = _haar_wavedec(q, M)
        cv = _haar_wavedec(v, M)
        prod = []
        for j in range(M):
            wq = weight_q[None, :, j, None, :]
            wv = weight_v[None, :, j, None, :]
            prod.append(cq[j] * wq * (cv[j] * wv))
        prod.append(cq[M] * cv[M])
        a = prod[0]
        for d in prod[1:]:
            a = _haar_idwt_step(a, d)
        out = a.transpose(0, 2, 1, 3).reshape(B, L, D)
        return out @ W_out.T + b_out

    def _L0_ffn_ref(x, gate_W, gate_b, W1, b1, W2, b2, ln_gamma, ln_beta):
        import jax, jax.numpy as jnp
        import numpy as np
        D = 128
        E = 8
        H = 256
        TOP_K = 2
        ALPHA = 0.5
        LN_EPS = 1e-05

        def _experts_all(x, W1, b1, W2, b2):
            h = jax.nn.relu(jnp.einsum('bld,edh->eblh', x, W1) + b1[:, None, None, :])
            return jnp.einsum('eblh,ehd->ebld', h, W2) + b2[:, None, None, :]

        def _selected_expert(x, expert_idx, W1, b1, W2, b2):
            oh = jax.nn.one_hot(expert_idx, E, dtype=x.dtype)
            return jnp.einsum('ebld,ble->bld', _experts_all(x, W1, b1, W2, b2), oh)

        def _layer_norm(x, gamma, beta):
            mu = jnp.mean(x, axis=-1, keepdims=True)
            var = jnp.mean(jnp.square(x - mu), axis=-1, keepdims=True)
            return (x - mu) * jax.lax.rsqrt(var + LN_EPS) * gamma + beta
        residual = x
        gate_logits = jnp.einsum('bld,de->ble', x, gate_W) + gate_b
        gate_weights = jax.nn.softmax(gate_logits, axis=-1)
        topk_vals, topk_idx = jax.lax.top_k(gate_weights, TOP_K)
        boost = jax.lax.stop_gradient(x)
        outs = []
        for i in range(TOP_K):
            eo = _selected_expert(boost, topk_idx[:, :, i], W1, b1, W2, b2)
            outs.append(eo)
            if i < TOP_K - 1:
                boost = boost + ALPHA * jax.lax.stop_gradient(eo)
        fused = sum((topk_vals[:, :, i:i + 1] * outs[i] for i in range(TOP_K)))
        return _layer_norm(residual + fused, ln_gamma, ln_beta)
    x = L0_attn_query
    xn = _layernorm(x, axis=-1)
    s = _L0_attn_ref(xn, L0_attn_W_qkv, L0_attn_b_qkv, L0_attn_W_out, L0_attn_b_out, L0_attn_weight_q, L0_attn_weight_v)
    g = _silu(_L0_ffn_ref(xn, L0_ffn_gate_W, L0_ffn_gate_b, L0_ffn_W1, L0_ffn_b1, L0_ffn_W2, L0_ffn_b2, L0_ffn_ln_gamma, L0_ffn_ln_beta))
    x = x + s * g
    return x

_drawn_inputs = setup_inputs


def setup_inputs(seed=0):
    import zlib

    import numpy as np

    out = dict(_drawn_inputs(seed))
    spreads = {'L0_attn_b_qkv': (0.0, 0.8),
     'L0_attn_b_out': (0.0, 0.1),
     'L0_ffn_gate_b': (0.0, 0.8),
     'L0_ffn_b1': (0.0, 0.8),
     'L0_ffn_b2': (0.0, 0.8),
     'L0_ffn_ln_gamma': (1.0, 0.6),
     'L0_ffn_ln_beta': (0.0, 0.8)}
    factors = {'L0_attn_W_qkv': 6.238,
     'L0_attn_W_out': 5.361,
     'L0_attn_weight_q': 7.125,
     'L0_attn_weight_v': 6.673,
     'L0_ffn_gate_W': 8.0,
     'L0_ffn_W1': 8.0,
     'L0_ffn_W2': 8.0}
    for name, (base, spread) in spreads.items():
        noise = np.random.default_rng([zlib.crc32(name.encode()), seed]).standard_normal(out[name].shape)
        drawn = base * np.exp(spread * noise) if base else spread * noise
        out[name] = jnp.asarray(drawn.astype(out[name].dtype))
    for name, factor in factors.items():
        out[name] = (out[name] * factor).astype(out[name].dtype)
    return out
```

```python
from contextlib import ExitStack

import numpy as np

import concourse.bass as bass
from concourse import mybir

F32 = mybir.dt.float32
BF16 = mybir.dt.bfloat16
I32 = mybir.dt.int32
U32 = mybir.dt.uint32
ALU = mybir.AluOpType
ACT = mybir.ActivationFunctionType
AX_X = mybir.AxisListType.X

P = 128
E = 8
H = 256
TOKENS = 16 * 256
TILES = TOKENS // P
GT = 8
GROUPS = TILES // GT
ST = 4
STEPS = TILES // ST
K = 2
REG = TOKENS + P
ROWS = (E + 1) * REG
EXPERT_TILES = TILES - 1 + E
RING = 8
ROW1 = P + 4
ROW2 = 2 * P + 2
NOWHERE = 1.0e6
EPS = 1e-5
C1 = 0.7071067811865476

INS = ["query", "wq_t", "wv_t", "bq", "bv", "wo_t", "bo", "weight_q", "weight_v", "gate_w", "gate_b", "w1", "w2",
       "b12", "gamma", "beta", "identity", "haar", "haar_t", "before", "tok", "pad1", "pad2", "tile_consts"]


def haar_matrix():
    c = np.float32(C1)
    m = np.zeros((P, P), np.float32)
    for k in range(P // 8):
        m[8 * k:8 * k + 8, k] = c * c * c
        m[8 * k:8 * k + 4, 16 + k] = c * c * c
        m[8 * k + 4:8 * k + 8, 16 + k] = -c * c * c
    for k in range(P // 4):
        m[4 * k:4 * k + 2, 32 + k] = c * c
        m[4 * k + 2:4 * k + 4, 32 + k] = -c * c
    for k in range(P // 2):
        m[2 * k, 64 + k] = c
        m[2 * k + 1, 64 + k] = -c
    return m


LEVELS = ((0, 16), (16, 32), (32, 64), (64, 128))


def consts():
    pad1 = np.zeros((P, ROW1), np.float32)
    pad1[:, P] = pad1[:, P + 3] = NOWHERE
    pad2 = np.zeros((P, ROW2), np.float32)
    pad2[:, 2 * P + 1] = NOWHERE
    p, t = np.arange(P), np.arange(TILES)
    line = np.concatenate([np.arange(E), np.tile(np.arange(E) * REG, K),
                           np.tril(np.ones((E, E))).ravel(), np.arange(EXPERT_TILES)]).astype(np.float32)
    return {
        "identity": np.eye(P, dtype=np.float32),
        "haar": haar_matrix(),
        "haar_t": np.ascontiguousarray(haar_matrix().T),
        "before": np.triu(np.ones((P, P), np.float32), 1),
        "tok": (t[None, :] * P + p[:, None]).astype(np.float32),
        "pad1": pad1, "pad2": pad2,
        "tile_consts": np.tile(line, (P, 1)),
    }


def build(nc, io, out):
    ctx = ExitStack()
    with ctx:
        def sb(name, shape, dt=F32):
            return ctx.enter_context(nc.sbuf_tensor(name, shape, dt))

        def sem(name):
            return ctx.enter_context(nc.semaphore(name))

        rows1_dram = nc.dram_tensor("rows1", [ROWS, ROW1], F32).ap()
        rows2_dram = nc.dram_tensor("rows2", [ROWS, ROW2], F32).ap()
        z_dram = nc.dram_tensor("z_by_token", [TOKENS, P], F32).ap()
        b_split_dram = nc.dram_tensor("b_split", [3, E, H + P], BF16).ap()

        wq, wv, wo = (sb(n, [P, P]) for n in ("wq", "wv", "wo"))
        bo_bc, gamma_bc, beta_bc = (sb(n, [P, P]) for n in ("bo_bc", "gamma_bc", "beta_bc"))
        gw = sb("gw", [P, E])
        gb_bc = sb("gb_bc", [P, E])
        att_cols = sb("att_cols", [P, 8])
        att_scale = sb("att_scale", [P, 6])
        ident, haar, haar_t = (sb(n, [P, P]) for n in ("ident", "haar_sb", "haar_t_sb"))
        before_f = sb("before_f", [P, P])
        before = sb("before_sb", [P, P], BF16)
        ones = sb("ones", [P, P], BF16)
        consts_sb = sb("consts_sb", [P, E + K * E + E * E + EXPERT_TILES])
        iota_e = consts_sb[:, 0:E]
        region = consts_sb[:, E:E + K * E]
        tril = consts_sb[:, E + K * E:E + K * E + E * E]
        iota_t = consts_sb[:, E + K * E + E * E:]
        pad1, pad2 = sb("pad1_sb", [P, ROW1]), sb("pad2_sb", [P, ROW2])
        eps_col = sb("eps_col", [P, 1])
        w2 = sb("w2_sb", [P, E * 2 * P])
        w1 = [sb(f"w1_{j}", [P, H]) for j in range(RING)]
        b_row = sb("b_row", [E, H + P])
        b_rest = sb("b_rest", [E, 2, H + P])
        b_part = sb("b_part", [E, 3, H + P], BF16)
        b_split = sb("b_split_sb", [P, E * (H + P)], BF16)

        x = sb("x", [P, TILES * P])
        s = sb("s", [P, TILES * P])
        tok = sb("tok_sb", [P, TILES])

        rows = [sb(f"rows_{b}", [P, GT, ROW1]) for b in range(2)]
        slot1 = [sb(f"slot1_{b}", [P, GT], I32) for b in range(2)]
        stats = sb("stats", [P, GT, 6])
        moments = sb("moments", [P, GT, 2])
        var = sb("var", [P, GT])
        half_bits = sb("half_bits", [P, GT], I32)
        rstd = sb("rstd", [P, GT])
        newton = sb("newton", [P, GT])
        xt = [sb(f"xt_{u}", [P, ST * P]) for u in range(2)]
        hx = [sb(f"hx_{u}", [P, ST * P]) for u in range(4)]
        logits = sb("logits", [P, GT, E])
        top = sb("top", [P, GT, 8])
        top_at = sb("top_at", [P, GT, 8], U32)
        onehot = sb("onehot", [P, GT, K, E], BF16)
        shifted = sb("shifted", [P, GT, E + 1])
        expd = sb("expd", [P, GT, E + 1])
        total = sb("total", [P, GT])
        places = sb("places", [P, GT, K * E])
        chosen = sb("chosen", [P, GT, K, E])
        slots = sb("slots", [P, GT, K])
        carry = sb("carry", [P, K * E])
        qw = [sb(f"qw_{b}", [P, ST * P]) for b in range(2)]
        prod = [sb(f"prod_{b}", [P, ST * P]) for b in range(2)]
        y_sb = [sb(f"y_sb_{b}", [P, ST * P]) for b in range(2)]

        counts = sb("counts", [1, K * E])
        counts_i = sb("counts_i", [1, K * E], I32)
        n_tiles = sb("n_tiles", [1, K * E])
        tri = sb("tri", [1, K, E, E])
        ends = sb("ends", [1, K, E])
        past = sb("past", [1, K, EXPERT_TILES, E])
        past_n = sb("past_n", [1, K, EXPERT_TILES, E])
        t_expert = sb("t_expert", [1, K, EXPERT_TILES])
        t_start = sb("t_start", [1, K, EXPERT_TILES])
        t_row = sb("t_row", [1, K, EXPERT_TILES])
        table = sb("table", [1, K * EXPERT_TILES * 4], I32)
        pad_at = sb("pad_at", [1, K * (E + 1)], I32)

        row_in = [sb(f"row_in_{j}", [P, ROW2]) for j in range(RING)]
        row_out = [sb(f"row_out_{j}", [P, ROW2]) for j in range(RING)]
        place = [sb(f"place_{j}", [P, 1], I32) for j in range(RING)]
        et = [sb(f"et_{b}", [P, P]) for b in range(2)]
        hid = [sb(f"hid_{b}", [P, 2 * P]) for b in range(2)]
        res = [sb(f"res_{b}", [P, P]) for b in range(2)]
        cent = [sb(f"cent_{b}", [P, P]) for b in range(2)]
        st2 = [sb(f"st2_{b}", [P, 6]) for b in range(2)]
        mv2 = [sb(f"mv2_{b}", [P, 2]) for b in range(2)]
        std2 = [sb(f"std2_{b}", [P, 1]) for b in range(2)]
        rstd2 = [sb(f"rstd2_{b}", [P, 1]) for b in range(2)]
        z = sb("z", [P, TILES * P])

        bank = [ctx.enter_context(nc.psum_tensor(f"bank{i}", [P, 512], F32)) for i in range(8)]
        ps_x, ps_lg, ps_rk, ps_q, ps_v, ps_y, ps_s = bank[0:2], bank[2], bank[3], bank[4], bank[5], bank[6], bank[7]
        ps_t, ps_h, ps_o = bank[0:2], bank[2:4], bank[4:6]

        x_in = [sem(f"x_in_{g}") for g in range(GROUPS)]
        const_in = sem("const_in")
        att_in = sem("att_in")
        late_in = sem("late_in")
        b_in = sem("b_in")
        zeroed = sem("zeroed")
        set_up = sem("set_up")
        b_parts = sem("b_parts")
        b_stored = sem("b_stored")
        b_loaded = sem("b_loaded")
        stats_done = sem("stats_done")
        moments_done = sem("moments_done")
        rstd_step = sem("rstd_step")
        xn_done = sem("xn_done")
        xt_psum = sem("xt_psum")
        xt_sbuf = sem("xt_sbuf")
        logits_psum = sem("logits_psum")
        logits_sbuf = sem("logits_sbuf")
        top_done = sem("top_done")
        top_at_done = sem("top_at_done")
        onehot_done = sem("onehot_done")
        shifted_done = sem("shifted_done")
        exp_done = sem("exp_done")
        total_done = sem("total_done")
        weight1_done = sem("weight1_done")
        rank_psum = sem("rank_psum")
        places_done = sem("places_done")
        carry_done = sem("carry_done")
        chosen_done = sem("chosen_done")
        slots_done = sem("slots_done")
        meta_done = sem("meta_done")
        sent = [[sem(f"sent_{b}_{t}") for t in range(GT)] for b in range(2)]
        hx_psum = sem("hx_psum")
        hx_sbuf = sem("hx_sbuf")
        q_psum = sem("q_psum")
        v_psum = sem("v_psum")
        qw_done = sem("qw_done")
        prod_done = sem("prod_done")
        y_psum = sem("y_psum")
        y_sbuf = sem("y_sbuf")
        s_psum = sem("s_psum")
        s_sbuf = sem("s_sbuf")
        table_step = sem("table_step")
        table_done = sem("table_done")
        pads1 = sem("pads1")
        pads2 = sem("pads2")

        class Pass:
            def __init__(self, k):
                self.k = k
                self.rows_in = [sem(f"p{k}_rows_in_{j}") for j in range(RING)]
                self.w1_in = [sem(f"p{k}_w1_in_{j}") for j in range(RING)]
                self.sent = [sem(f"p{k}_sent_{j}") for j in range(RING)]
                self.et_psum = sem(f"p{k}_et_psum")
                self.et_sbuf = sem(f"p{k}_et_sbuf")
                self.hid_psum = sem(f"p{k}_hid_psum")
                self.hid_sbuf = sem(f"p{k}_hid_sbuf")
                self.o_psum = sem(f"p{k}_o_psum")
                self.o_read = sem(f"p{k}_o_read")
                self.row_done = sem(f"p{k}_row_done")
                self.scattering = sem(f"p{k}_scattering")
                self.stats = sem(f"p{k}_stats")
                self.moments = sem(f"p{k}_moments")
                self.std = sem(f"p{k}_std")
                self.rstd = sem(f"p{k}_rstd")
                self.cent = sem(f"p{k}_cent")

        passes = [Pass(0), Pass(1)]
        z_in = [sem(f"z_in_{n}") for n in range(STEPS)]
        silu_done = sem("silu_done")
        gated = sem("gated")
        out_done = sem("out_done")
        out_stored = sem("out_stored")

        query_v = io["query"].rearrange("b l d -> (b l) d").rearrange("(t p) d -> p t d", p=P)
        out_v = out.rearrange("b l d -> (b l) d").rearrange("(t p) d -> p t d", p=P)
        z_v = z_dram.rearrange("(t p) d -> p t d", p=P)

        def cols(ap, t, n=1):
            return ap[:, t * P:(t + n) * P]

        def by_tile(ap, n):
            return ap.rearrange("p (t c) -> p t c", t=n)

        def tiles(eng, first, step):
            loops = (EXPERT_TILES - first) // RING
            with eng.Fori(0, loops) as i:
                for k in range(first, first + RING):
                    step(i * RING + k, i + k // RING, k % RING)
            for t in range(first + loops * RING, EXPERT_TILES):
                step(t, t // RING, t % RING)

        block = ctx.enter_context(nc.Block())

        @block.sync
        def _(sp):
            sp.dma_start(by_tile(cols(x, 0, GT), GT), query_v[:, 0:GT, :]).then_inc(x_in[0], 16)
            first = [(ident[:, :], io["identity"]), (gw[:, :], io["gate_w"]),
                     (gb_bc[:, :], io["gate_b"].rearrange("(a n) -> a n", a=1).to_broadcast([P, E])),
                     (haar[:, :], io["haar"]), (before_f[:, :], io["before"]), (consts_sb[:, :], io["tile_consts"]),
                     (tok[:, :], io["tok"])]
            for dst, src in first:
                sp.dma_start(dst, src).then_inc(const_in, 16)
            for g in range(1, GROUPS):
                sp.dma_start(by_tile(cols(x, g * GT, GT), GT), query_v[:, g * GT:(g + 1) * GT, :])\
                    .then_inc(x_in[g], 16)
            sp.wait_ge(b_parts, 5)
            for k in range(3):
                sp.dma_start(b_split_dram[k], b_part[:, k, :]).then_inc(b_stored, 16)
            sp.wait_ge(b_stored, 48)
            sp.wait_ge(zeroed, 1)
            sp.dma_start(b_split[0:3, :], b_split_dram.rearrange("k e n -> k (e n)")).then_inc(b_loaded, 16)
            sp.wait_ge(table_done, 1)
            sp.wait_ge(late_in, 16 * 5)
            with sp.Fori(0, E + 1) as e:
                at = sp.value_load(pad_at[0:1, bass.ds(e, 1)], min_val=0, max_val=E * REG)
                sp.dma_start(rows1_dram[bass.ds(at, P), :], pad1[:, :]).then_inc(pads1, 16)

            for ps in passes:
                src, width = (rows1_dram, ROW1) if ps.k == 0 else (rows2_dram, ROW2)

                def tile_entry(t):
                    at = (t + ps.k * EXPERT_TILES) * 4
                    row = sp.value_load(table[0:1, bass.ds(at, 1)], min_val=0, max_val=E * REG)
                    expert = sp.value_load(table[0:1, bass.ds(at + 1, 1)], min_val=0, max_val=E - 1)
                    return row, expert

                def load_w1(expert, j):
                    sp.dma_start(w1[j][:, :], io["w1"][bass.ds(expert, 1), :, :].rearrange("e p h -> p (e h)"))\
                        .then_inc(ps.w1_in[j], 16)

                def load_rows(row, j):
                    sp.dma_start(row_in[j][:, 0:width], src[bass.ds(row, P), :]).then_inc(ps.rows_in[j], 16)

                if ps.k == 1:
                    sp.wait_ge(passes[0].hid_psum, EXPERT_TILES)
                    sp.wait_ge(table_done, 2)
                entries = []
                for t in range(RING):
                    row, expert = tile_entry(t)
                    entries.append(row)
                    load_w1(expert, t)
                if ps.k == 0:
                    for g in range(GROUPS - 2, GROUPS):
                        for t in range(GT):
                            sp.wait_ge(sent[g % 2][t], 16 * (g // 2 + 1))
                    sp.wait_ge(pads1, 16 * (E + 1))
                else:
                    for j in range(RING):
                        sp.wait_ge(passes[0].sent[j], 16 * len(range(j, EXPERT_TILES, RING)))
                    sp.wait_ge(pads2, 16 * (E + 1))
                    sp.wait_ge(passes[0].row_done, EXPERT_TILES)
                for t in range(RING):
                    load_rows(entries[t], t)

                def step(t, turn, j):
                    row, expert = tile_entry(t)
                    sp.wait_ge(ps.hid_psum, t - RING + 1)
                    load_w1(expert, j)
                    sp.wait_ge(ps.row_done, t - RING + 1)
                    load_rows(row, j)

                tiles(sp, RING, step)

            for j in range(RING):
                sp.wait_ge(passes[1].sent[j], 16 * len(range(j, EXPERT_TILES, RING)))
            for n in range(STEPS):
                sp.dma_start(by_tile(cols(z, n * ST, ST), ST), z_v[:, n * ST:(n + 1) * ST, :]).then_inc(z_in[n], 16)
            for n in range(STEPS):
                sp.wait_ge(out_done, n + 1)
                sp.dma_start(out_v[:, n * ST:(n + 1) * ST, :], by_tile(cols(z, n * ST, ST), ST))\
                    .then_inc(out_stored, 16)
            sp.wait_ge(out_stored, 16 * STEPS)

        @block.gpsimd
        def _(pool):
            pool.memset(b_split[:, :].bitcast(I32), 0).then_inc(zeroed, 1)
            pool.memset(ones[:, :], 1.0).then_inc(zeroed, 1)
            pool.memset(eps_col[:, :], EPS).then_inc(zeroed, 1)
            for g in range(GROUPS):
                pool.wait_ge(meta_done, g + 1)
                for t in range(GT):
                    pool.indirect_dma_start(
                        out=rows1_dram[:, :], out_offset=bass.IndirectOffsetOnAxis(ap=slot1[g % 2][:, t:t + 1], axis=0),
                        in_=rows[g % 2][:, t, :], in_offset=None,
                        bounds_check=ROWS - 1, oob_is_err=False).then_inc(sent[g % 2][t], 16)
            for ps in passes:
                dst, width, last = (rows2_dram, ROW2, ROWS - 1) if ps.k == 0 else (z_dram, P, TOKENS - 1)

                def step(t, turn, j):
                    pool.wait_ge(ps.row_done, t + 1)
                    pool.sem_inc(ps.scattering, 1)
                    pool.indirect_dma_start(
                        out=dst[:, :], out_offset=bass.IndirectOffsetOnAxis(ap=place[j][:, 0:1], axis=0),
                        in_=row_out[j][:, 0:width], in_offset=None,
                        bounds_check=last, oob_is_err=False).then_inc(ps.sent[j], 16)

                tiles(pool, 0, step)

        @block.tensor
        def _(pe):
            def transposes(g):
                for u in range(2):
                    if g:
                        pe.wait_ge(hx_sbuf, 2 * (g - 1) + u + 1)
                    for t in range(ST):
                        pe.wait_ge(xn_done, GT * g + ST * u + t + 1)
                        mm = pe.transpose(cols(ps_x[u], t), rows[g % 2][:, ST * u + t, 0:P], ident[:, :])
                    mm.then_inc(xt_psum, 1)

            def gate(g):
                if g:
                    pe.wait_ge(logits_sbuf, g)
                for u in range(2):
                    pe.wait_ge(xt_sbuf, 2 * g + u + 1)
                    for t in range(ST):
                        at = (ST * u + t) * E
                        mm = pe.matmul(ps_lg[:, at:at + E], cols(xt[u], t), gw[:, :], start=True, stop=True)
                mm.then_inc(logits_psum, 1)

            def haar_coefs(g):
                for u in range(2):
                    pe.wait_ge(xt_sbuf, 2 * g + u + 1)
                    for t in range(ST):
                        mm = pe.matmul(cols(ps_x[u], t), rows[g % 2][:, ST * u + t, 0:P], haar[:, :],
                                       start=True, stop=True)
                    mm.then_inc(hx_psum, 1)

            def ranks(g):
                pe.wait_ge(onehot_done, g + 1)
                if g:
                    pe.wait_ge(carry_done, g)
                    pe.wait_ge(places_done, g)
                oh = onehot[:, :, :, :].rearrange("p t k e -> p t (k e)")
                n = K * E
                for t in range(GT):
                    pe.matmul(ps_rk[:, GT * n:GT * n + n], ones[:, :], oh[:, t, :], start=(t == 0), stop=(t == GT - 1))
                mm = pe.matmul(ps_rk[:, 0:GT * n], before[:, :], oh.rearrange("p t n -> p (t n)"),
                               start=True, stop=False, skip_group_check=True)
                for t in range(GT - 1):
                    later = GT - 1 - t
                    mm = pe.matmul(ps_rk[:, (t + 1) * n:GT * n].rearrange("p (t n) -> p t n", t=later), ones[:, :],
                                   oh[:, t:t + 1, :].to_broadcast([P, later, n]), start=False,
                                   stop=(t == GT - 2), skip_group_check=True)
                mm.then_inc(rank_psum, 1)

            def q_of(n):
                if n:
                    pe.wait_ge(qw_done, n)
                pe.wait_ge(hx_sbuf, n + 1)
                pe.matmul(ps_q[:, :], wq[:, :], hx[n % 4][:, :], start=True, stop=True).then_inc(q_psum, 1)

            def v_of(n):
                if n:
                    pe.wait_ge(prod_done, n)
                pe.matmul(ps_v[:, :], wv[:, :], hx[n % 4][:, :], start=True, stop=True).then_inc(v_psum, 1)

            def y_of(n):
                pe.wait_ge(prod_done, n + 1)
                if n:
                    pe.wait_ge(y_sbuf, n)
                for t in range(ST):
                    mm = pe.matmul(cols(ps_y, t), cols(prod[n % 2], t), wo[:, :], start=True, stop=True)
                mm.then_inc(y_psum, 1)

            def s_of(n):
                pe.wait_ge(y_sbuf, n + 1)
                if n:
                    pe.wait_ge(s_sbuf, n)
                pe.matmul(ps_s[:, :], haar_t[:, :], y_sb[n % 2][:, :], start=True, stop=True).then_inc(s_psum, 1)

            def attention(n):
                if n < STEPS:
                    q_of(n)
                if n:
                    y_of(n - 1)
                if n < STEPS:
                    v_of(n)
                if n:
                    s_of(n - 1)

            pe.wait_ge(const_in, 16 * 7)
            pe.wait_ge(set_up, 1)
            for g in range(GROUPS):
                transposes(g)
                gate(g)
                haar_coefs(g)
                if g == 0:
                    pe.wait_ge(zeroed, 3)
                    ranks(g)
                    pe.wait_ge(att_in, 16 * 8)
                else:
                    attention(2 * g - 2)
                    ranks(g)
                    attention(2 * g - 1)
            attention(STEPS - 2)
            attention(STEPS - 1)
            attention(STEPS)

            pe.wait_ge(b_loaded, 16)
            pe.wait_ge(late_in, 16 * 5)
            pe.wait_ge(s_sbuf, STEPS)
            for ps in passes:
                def turn_rows(t, turn, j):
                    pe.wait_ge(ps.rows_in[j], 16 * (turn + 1))
                    pe.transpose(ps_t[t_par(j)][:, 0:P], row_in[j][:, 0:P], ident[:, :]).then_inc(ps.et_psum, 1)

                def t_par(j):
                    return j % 2

                def layer1(t, turn, j, expert, fresh):
                    pe.wait_ge(ps.et_sbuf, t + 1)
                    pe.wait_ge(ps.w1_in[j], 16 * (turn + 1))
                    if not fresh:
                        pe.wait_ge(ps.hid_sbuf, t - 1)
                    for c in range(2):
                        o = cols(ps_h[j % 2], c)
                        pe.matmul(o, cols(w1[j], c), et[j % 2][:, :], start=True, stop=False)
                        mm = pe.matmul(o, b_split[:, bass.ds(expert * (H + P) + c * P, P)], ones[:, :],
                                       start=False, stop=True)
                    mm.then_inc(ps.hid_psum, 1)

                def layer2(t, j, expert, fresh):
                    pe.wait_ge(ps.hid_sbuf, t + 1)
                    if not fresh:
                        pe.wait_ge(ps.o_read, t - 1)
                    o = ps_o[j % 2][:, 0:P]
                    for c in range(2):
                        pe.matmul(o, cols(hid[j % 2], c), w2[:, bass.ds(expert * 2 * P + c * P, P)],
                                  start=(c == 0), stop=False)
                    pe.matmul(o, ones[:, :], b_split[:, bass.ds(expert * (H + P) + H, P)],
                              start=False, stop=True).then_inc(ps.o_psum, 1)

                def expert_of(t):
                    at = (t + ps.k * EXPERT_TILES) * 4 + 1
                    return pe.value_load(table[0:1, bass.ds(at, 1)], min_val=0, max_val=E - 1)

                pe.wait_ge(table_done, ps.k + 1)
                turn_rows(0, 0, 0)
                turn_rows(1, 0, 1)
                layer1(0, 0, 0, expert_of(0), True)
                turn_rows(2, 0, 2)

                def step(t, turn, j, fresh1=False, fresh2=False, ahead=True):
                    layer1(t, turn, j, expert_of(t), fresh1)
                    if ahead:
                        turn_rows(t + 2, turn + (j + 2) // RING, (j + 2) % RING)
                    layer2(t - 1, (j - 1) % RING, expert_of(t - 1), fresh2)

                step(1, 0, 1, fresh1=True, fresh2=True)
                step(2, 0, 2, fresh2=True)
                loops = (EXPERT_TILES - 5) // RING
                with pe.Fori(0, loops) as i:
                    for k in range(3, 3 + RING):
                        step(i * RING + k, i + k // RING, k % RING)
                for t in range(3 + loops * RING, EXPERT_TILES):
                    step(t, t // RING, t % RING, ahead=t + 2 < EXPERT_TILES)
                t = EXPERT_TILES - 1
                layer2(t, t % RING, expert_of(t), False)

        @block.scalar
        def _(act):
            loads = [(wq[:, :], io["wq_t"]), (wv[:, :], io["wv_t"]), (wo[:, :], io["wo_t"]),
                     (haar_t[:, :], io["haar_t"]),
                     (att_cols[:, 0:1], io["bq"].rearrange("(p a) -> p a", a=1)),
                     (att_cols[:, 1:2], io["bv"].rearrange("(p a) -> p a", a=1)),
                     (att_cols[:, 2:5], io["weight_q"]), (att_cols[:, 5:8], io["weight_v"])]
            for dst, src in loads:
                act.dma_start(dst, src).then_inc(att_in, 16)
            act.dma_start(b_row[:, :], io["b12"]).then_inc(b_in, 16)
            act.dma_start(bo_bc[:, :], io["bo"].rearrange("(a n) -> a n", a=1).to_broadcast([P, P])).then_inc(b_in, 16)

            def xt_copy(g):
                for u in range(2):
                    act.wait_ge(xt_psum, 2 * g + u + 1)
                    if g:
                        act.wait_ge(logits_psum, g)
                    act.activation(xt[u][:, :], ps_x[u][:, :], ACT.Copy).then_inc(xt_sbuf, 1)

            def hx_copy(g):
                for u in range(2):
                    n = 2 * g + u
                    act.wait_ge(hx_psum, n + 1)
                    if n >= 4:
                        act.wait_ge(v_psum, n - 3)
                    act.activation(hx[n % 4][:, :], ps_x[u][:, :], ACT.Copy).then_inc(hx_sbuf, 1)

            def exps(g):
                act.wait_ge(shifted_done, g + 1)
                if g:
                    act.wait_ge(weight1_done, 2 * g)
                act.activation(expd[:, :, :], shifted[:, :, :], ACT.Exp).then_inc(exp_done, 1)

            def qw_of(n):
                act.wait_ge(q_psum, n + 1)
                if n >= 2:
                    act.wait_ge(prod_done, n - 1)
                src, dst = by_tile(ps_q[:, :], ST), by_tile(qw[n % 2][:, :], ST)
                for k, (a, b) in enumerate(LEVELS):
                    if k == 0:
                        ins = act.activation(dst[:, :, a:b], src[:, :, a:b], ACT.Identity,
                                             bias=att_scale[:, 0:1], scale=att_scale[:, 2:3])
                    elif k < 3:
                        ins = act.activation(dst[:, :, a:b], src[:, :, a:b], ACT.Copy, scale=att_scale[:, 2 + k:3 + k])
                    else:
                        ins = act.activation(dst[:, :, a:b], src[:, :, a:b], ACT.Copy)
                ins.then_inc(qw_done, 1)

            def y_copy(n):
                act.wait_ge(y_psum, n + 1)
                if n >= 2:
                    act.wait_ge(s_psum, n - 1)
                act.activation(y_sb[n % 2][:, :], ps_y[:, :], ACT.Copy).then_inc(y_sbuf, 1)

            def attention(n):
                if n < STEPS:
                    qw_of(n)
                if n:
                    y_copy(n - 1)

            for g in range(GROUPS):
                xt_copy(g)
                hx_copy(g)
                exps(g)
                if g == 0:
                    late = [(w2[:, :].rearrange("p (e c d) -> p e c d", e=E, c=2),
                             io["w2"].rearrange("e (c p) d -> p e c d", p=P)),
                            (pad1[:, :], io["pad1"]), (pad2[:, :], io["pad2"]),
                            (gamma_bc[:, :], io["gamma"].rearrange("(a n) -> a n", a=1).to_broadcast([P, P])),
                            (beta_bc[:, :], io["beta"].rearrange("(a n) -> a n", a=1).to_broadcast([P, P]))]
                    for dst, src in late:
                        act.dma_start(dst, src).then_inc(late_in, 16)
                    act.wait_ge(set_up, 4)
                else:
                    attention(2 * g - 2)
                    attention(2 * g - 1)
            attention(STEPS - 2)
            act.wait_ge(table_done, 1)
            act.wait_ge(late_in, 16 * 5)
            with act.Fori(0, E + 1) as e:
                at = act.value_load(pad_at[0:1, bass.ds(e + E + 1, 1)], min_val=0, max_val=E * REG)
                act.dma_start(rows2_dram[bass.ds(at, P), :], pad2[:, :]).then_inc(pads2, 16)
            attention(STEPS - 1)
            attention(STEPS)

            for ps in passes:
                def turned(t, j, fresh=False):
                    act.wait_ge(ps.et_psum, t + 1)
                    if not fresh:
                        act.wait_ge(ps.hid_psum, t - 1)
                    act.activation(et[j % 2][:, :], ps_t[j % 2][:, 0:P], ACT.Copy).then_inc(ps.et_sbuf, 1)

                def relu(t, j, fresh=False):
                    act.wait_ge(ps.hid_psum, t + 1)
                    if not fresh:
                        act.wait_ge(ps.o_psum, t - 1)
                    act.activation(hid[j % 2][:, :], ps_h[j % 2][:, 0:2 * P], ACT.Relu).then_inc(ps.hid_sbuf, 1)

                def deviation(t, j, fresh=False):
                    act.wait_ge(ps.moments, t + 1)
                    if not fresh:
                        act.wait_ge(ps.rstd, t - 1)
                    act.activation(std2[j % 2][:, :], mv2[j % 2][:, 1:2], ACT.Sqrt, bias=eps_col[:, 0:1])\
                        .then_inc(ps.std, 1)

                def step(t, turn, j, ahead=True, fresh=False, dev=True, dev_fresh=False):
                    relu(t, j, fresh)
                    if ahead:
                        turned(t + 2, (j + 2) % RING)
                    if ps.k == 1 and dev:
                        deviation(t - 2, (j - 2) % RING, dev_fresh)

                if ps.k == 1:
                    act.activation(std2[0][:, :], eps_col[:, 0:1], ACT.Sqrt)
                turned(0, 0, True)
                turned(1, 1, True)
                step(0, 0, 0, fresh=True, dev=False)
                step(1, 0, 1, fresh=True, dev=False)
                step(2, 0, 2, dev_fresh=True)
                step(3, 0, 3, dev_fresh=True)
                loops = (EXPERT_TILES - 6) // RING
                with act.Fori(0, loops) as i:
                    for k in range(4, 4 + RING):
                        step(i * RING + k, i + k // RING, k % RING)
                for t in range(4 + loops * RING, EXPERT_TILES):
                    step(t, t // RING, t % RING, ahead=t + 2 < EXPERT_TILES)
                if ps.k == 1:
                    for t in range(EXPERT_TILES - 2, EXPERT_TILES):
                        deviation(t, t % RING)

            for n in range(STEPS):
                act.wait_ge(z_in[n], 16)
                act.activation(cols(z, n * ST, ST), cols(z, n * ST, ST), ACT.Silu).then_inc(silu_done, 1)

        @block.vector
        def _(dve):
            rstd_steps = [0]

            def rstd_next(ins):
                rstd_steps[0] += 1
                ins.then_inc(rstd_step, 1)
                dve.wait_ge(rstd_step, rstd_steps[0])

            def layer_norm(g):
                dve.wait_ge(x_in[g], 16)
                for t in range(GT):
                    ins = dve.bn_stats(stats[:, t, :], cols(x, GT * g + t))
                ins.then_inc(stats_done, 1)
                dve.wait_ge(stats_done, g + 1)
                for t in range(GT):
                    ins = dve.bn_aggr(moments[:, t, :], stats[:, t, :])
                ins.then_inc(moments_done, 1)
                dve.wait_ge(moments_done, g + 1)
                rstd_next(dve.tensor_scalar(var[:, :], moments[:, :, 1], EPS, None, ALU.add))
                rstd_next(dve.tensor_scalar(half_bits[:, :], var[:, :].bitcast(I32), 1, None,
                                            ALU.logical_shift_right))
                rstd_next(dve.tensor_scalar(rstd[:, :].bitcast(I32), half_bits[:, :], -1.0, float(0x5f3759df),
                                            ALU.mult, ALU.add))
                for _ in range(3):
                    rstd_next(dve.tensor_tensor(newton[:, :], rstd[:, :], rstd[:, :], ALU.mult))
                    rstd_next(dve.scalar_tensor_tensor(newton[:, :], newton[:, :], -0.5, var[:, :],
                                                       ALU.mult, ALU.mult))
                    rstd_next(dve.scalar_tensor_tensor(rstd[:, :], newton[:, :], 1.5, rstd[:, :],
                                                       ALU.add, ALU.mult))
                for t in range(GT):
                    if g >= 2:
                        dve.wait_ge(sent[g % 2][t], 16 * (g // 2))
                        dve.wait_ge(hx_psum, 2 * g - 2)
                    dve.tensor_scalar(rows[g % 2][:, t, 0:P], cols(x, GT * g + t), moments[:, t, 0:1],
                                      rstd[:, t:t + 1], ALU.subtract, ALU.mult).then_inc(xn_done, 1)

            def route(g):
                dve.wait_ge(logits_psum, g + 1)
                dve.tensor_tensor(logits[:, :, :], ps_lg[:, 0:GT * E].rearrange("p (t e) -> p t e", t=GT),
                                  gb_bc[:, None, :].to_broadcast([P, GT, E]), ALU.add).then_inc(logits_sbuf, 1)
                dve.wait_ge(logits_sbuf, g + 1)
                for t in range(GT):
                    ins = dve.max(top[:, t, :], logits[:, t, :])
                ins.then_inc(top_done, 1)
                dve.wait_ge(top_done, g + 1)
                for t in range(GT):
                    ins = dve.max_index(top_at[:, t, :], top[:, t, :], logits[:, t, :])
                ins.then_inc(top_at_done, 1)
                dve.tensor_tensor(shifted[:, :, 0:E], logits[:, :, :], top[:, :, 0:1].to_broadcast([P, GT, E]),
                                  ALU.subtract)
                dve.tensor_tensor(shifted[:, :, E], top[:, :, 1], top[:, :, 0], ALU.subtract)\
                    .then_inc(shifted_done, 1)
                dve.wait_ge(top_at_done, g + 1)
                if g:
                    dve.wait_ge(rank_psum, g)
                dve.tensor_tensor(onehot[:, :, :, :],
                                  iota_e[:, None, None, :].to_broadcast([P, GT, K, E]),
                                  top_at[:, :, 0:K][:, :, :, None].to_broadcast([P, GT, K, E]), ALU.is_equal)\
                    .then_inc(onehot_done, 1)

            def weights(g):
                dve.wait_ge(exp_done, g + 1)
                dve.tensor_reduce(total[:, :], expd[:, :, 0:E], AX_X, ALU.add).then_inc(total_done, 1)
                dve.wait_ge(total_done, g + 1)
                dve.reciprocal(rows[g % 2][:, :, P + 1], total[:, :]).then_inc(weight1_done, 1)
                dve.wait_ge(weight1_done, 2 * g + 1)
                dve.tensor_tensor(rows[g % 2][:, :, P + 2], expd[:, :, E], rows[g % 2][:, :, P + 1], ALU.mult)\
                    .then_inc(weight1_done, 1)

            def place_rows(g):
                dve.wait_ge(rank_psum, g + 1)
                n = K * E
                dve.tensor_tensor(places[:, :, :], ps_rk[:, 0:GT * n].rearrange("p (t n) -> p t n", t=GT),
                                  carry[:, None, :].to_broadcast([P, GT, n]), ALU.add).then_inc(places_done, 1)
                dve.wait_ge(places_done, g + 1)
                dve.tensor_tensor(carry[:, :], carry[:, :], ps_rk[:, GT * n:GT * n + n], ALU.add)\
                    .then_inc(carry_done, 1)
                dve.tensor_tensor(chosen[:, :, :, :], places[:, :, :].rearrange("p t (k e) -> p t k e", k=K),
                                  onehot[:, :, :, :], ALU.mult).then_inc(chosen_done, 1)
                dve.wait_ge(chosen_done, g + 1)
                dve.tensor_reduce(slots[:, :, :], chosen[:, :, :, :], AX_X, ALU.add).then_inc(slots_done, 1)
                dve.tensor_copy(rows[g % 2][:, :, P + 3], tok[:, g * GT:(g + 1) * GT])
                dve.wait_ge(slots_done, g + 1)
                dve.tensor_copy(rows[g % 2][:, :, P], slots[:, :, 1])
                dve.tensor_copy(slot1[g % 2][:, :], slots[:, :, 0]).then_inc(meta_done, 1)

            def attention(n):
                if n < STEPS:
                    dve.wait_ge(v_psum, n + 1)
                    dve.wait_ge(qw_done, n + 1)
                    if n >= 2:
                        dve.wait_ge(y_psum, n - 1)
                    v, q, o = (by_tile(a[:, :], ST) for a in (ps_v, qw[n % 2], prod[n % 2]))
                    b = LEVELS[0][1]
                    dve.scalar_tensor_tensor(o[:, :, 0:b], v[:, :, 0:b], att_scale[:, 1:2], q[:, :, 0:b],
                                             ALU.add, ALU.mult)
                    dve.tensor_tensor(o[:, :, b:P], v[:, :, b:P], q[:, :, b:P], ALU.mult).then_inc(prod_done, 1)
                if n:
                    dve.wait_ge(s_psum, n)
                    dve.tensor_tensor(by_tile(cols(s, (n - 1) * ST, ST), ST), by_tile(ps_s[:, :], ST),
                                      bo_bc[:, None, :].to_broadcast([P, ST, P]), ALU.add).then_inc(s_sbuf, 1)

            table_steps = [0]

            def table_next(ins):
                table_steps[0] += 1
                ins.then_inc(table_step, 1)
                dve.wait_ge(table_step, table_steps[0])

            def tile_counts():
                dve.wait_ge(carry_done, GROUPS)
                dve.tensor_copy(pad_at[0:1, :].rearrange("a (k e) -> a k e", k=K)[:, :, 0:E],
                                carry[0:1, :].rearrange("a (k e) -> a k e", k=K))
                dve.memset(pad_at[0:1, :].rearrange("a (k e) -> a k e", k=K)[:, :, E], E * REG)
                table_next(dve.tensor_tensor(counts[:, :], carry[0:1, :], region[0:1, :], ALU.subtract))
                table_next(dve.tensor_scalar(counts_i[:, :], counts[:, :], float(P - 1), None, ALU.add))
                table_next(dve.tensor_scalar(counts_i[:, :], counts_i[:, :], 7, None, ALU.logical_shift_right))
                table_next(dve.tensor_copy(n_tiles[:, :], counts_i[:, :]))
                for k in range(K):
                    nt = n_tiles[:, k * E:(k + 1) * E]
                    table_next(dve.tensor_tensor(tri[:, k, :, :], tril[0:1, :].rearrange("a (i j) -> a i j", i=E),
                                                 nt[:, None, :].to_broadcast([1, E, E]), ALU.mult))
                    table_next(dve.tensor_reduce(ends[:, k, :], tri[:, k, :, :], AX_X, ALU.add))

            def tile_table(k):
                shape = [1, EXPERT_TILES, E]
                nt = n_tiles[:, k * E:(k + 1) * E]
                it = iota_t[0:1, :]
                table_next(dve.tensor_tensor(past[:, k], it[:, :, None].to_broadcast(shape),
                                             ends[:, k:k + 1, :].to_broadcast(shape), ALU.is_ge))
                dve.tensor_reduce(t_expert[:, k, :], past[:, k], AX_X, ALU.add)
                table_next(dve.tensor_tensor(past_n[:, k], past[:, k], nt[:, None, :].to_broadcast(shape), ALU.mult))
                table_next(dve.tensor_reduce(t_start[:, k, :], past_n[:, k], AX_X, ALU.add))
                table_next(dve.scalar_tensor_tensor(t_row[:, k, :], t_expert[:, k, :], float(REG // P), it,
                                                    ALU.mult, ALU.add))
                table_next(dve.tensor_tensor(t_row[:, k, :], t_row[:, k, :], t_start[:, k, :], ALU.subtract))
                entry = table[0:1, k * EXPERT_TILES * 4:(k + 1) * EXPERT_TILES * 4].rearrange("a (t n) -> a t n", n=4)
                dve.tensor_scalar(entry[:, :, 0], t_row[:, k, :], float(P), float(E * REG), ALU.mult, ALU.min)
                dve.tensor_scalar(entry[:, :, 1], t_expert[:, k, :], float(E - 1), None, ALU.min)\
                    .then_inc(table_done, 1)

            dve.wait_ge(const_in, 16 * 7)
            dve.tensor_copy(before[:, :], before_f[:, :])
            dve.tensor_copy(carry[:, :], region).then_inc(set_up, 1)
            layer_norm(0)
            route(0)
            dve.wait_ge(att_in, 16 * 8)
            dve.tensor_tensor(att_scale[:, 2:5], att_cols[:, 2:5], att_cols[:, 5:8], ALU.mult).then_inc(set_up, 1)
            dve.tensor_scalar(att_scale[:, 1:2], att_cols[:, 1:2], 8 * C1 ** 3, None, ALU.mult).then_inc(set_up, 1)
            weights(0)
            dve.wait_ge(set_up, 3)
            dve.scalar_tensor_tensor(att_scale[:, 0:1], att_cols[:, 0:1], 8 * C1 ** 3, att_scale[:, 2:3],
                                     ALU.mult, ALU.mult).then_inc(set_up, 1)
            place_rows(0)
            dve.wait_ge(b_in, 32)
            dve.tensor_copy(b_part[:, 0, :], b_row[:, :]).then_inc(b_parts, 1)
            dve.wait_ge(b_parts, 1)
            dve.tensor_tensor(b_rest[:, 0, :], b_row[:, :], b_part[:, 0, :], ALU.subtract).then_inc(b_parts, 1)
            dve.wait_ge(b_parts, 2)
            dve.tensor_copy(b_part[:, 1, :], b_rest[:, 0, :]).then_inc(b_parts, 1)
            dve.wait_ge(b_parts, 3)
            dve.tensor_tensor(b_rest[:, 1, :], b_rest[:, 0, :], b_part[:, 1, :], ALU.subtract).then_inc(b_parts, 1)
            dve.wait_ge(b_parts, 4)
            dve.tensor_copy(b_part[:, 2, :], b_rest[:, 1, :]).then_inc(b_parts, 1)
            for g in range(1, GROUPS):
                layer_norm(g)
                route(g)
                weights(g)
                attention(2 * g - 2)
                place_rows(g)
                if g == GROUPS - 1:
                    tile_counts()
                    tile_table(0)
                attention(2 * g - 1)
            tile_table(1)
            attention(STEPS - 2)
            attention(STEPS - 1)
            attention(STEPS)

            ps = passes[0]

            def step1(t, turn, j, fresh=False):
                a, b = row_in[j], row_out[j]
                if not fresh:
                    dve.wait_ge(ps.sent[j], 16 * turn)
                dve.wait_ge(ps.o_psum, t + 1)
                eo = ps_o[j % 2][:, 0:P]
                dve.scalar_tensor_tensor(b[:, 0:P], eo, 0.5, a[:, 0:P], ALU.mult, ALU.add)
                dve.scalar_tensor_tensor(b[:, P:2 * P], eo, a[:, P + 1:P + 2], a[:, 0:P], ALU.mult, ALU.add)\
                    .then_inc(ps.o_read, 1)
                dve.tensor_copy(b[:, 2 * P:2 * P + 2], a[:, P + 2:P + 4])
                dve.tensor_copy(place[j][:, :], a[:, P:P + 1]).then_inc(ps.row_done, 1)

            for t in range(RING):
                step1(t, 0, t, fresh=True)
            tiles(dve, RING, step1)

            ps2 = passes[1]

            def mix(t, turn, j, tail):
                a, c = row_in[j], j % 2
                dve.wait_ge(ps2.o_psum, t + 1)
                dve.scalar_tensor_tensor(res[c][:, :], ps_o[c][:, 0:P], a[:, 2 * P:2 * P + 1], a[:, P:2 * P],
                                         ALU.mult, ALU.add).then_inc(ps2.o_read, 1)
                if tail:
                    tail[0]()
                dve.wait_ge(ps2.o_read, t + 1)
                dve.bn_stats(st2[c][:, :], res[c][:, :]).then_inc(ps2.stats, 1)
                dve.wait_ge(ps2.stats, t + 1)
                if tail:
                    tail[1]()
                dve.bn_aggr(mv2[c][:, :], st2[c][:, :]).then_inc(ps2.moments, 1)
                if tail:
                    tail[2]()

            def tail_of(t, turn, j, fresh=False):
                a, b, c = row_in[j], row_out[j], j % 2

                def centre():
                    dve.wait_ge(ps2.moments, t + 1)
                    dve.scalar_tensor_tensor(cent[c][:, :], res[c][:, :], mv2[c][:, 0:1], gamma_bc[:, :],
                                             ALU.subtract, ALU.mult).then_inc(ps2.cent, 1)

                def invert():
                    dve.wait_ge(ps2.std, t + 1)
                    dve.reciprocal(rstd2[c][:, :], std2[c][:, :]).then_inc(ps2.rstd, 1)

                def finish():
                    if not fresh:
                        dve.wait_ge(ps2.sent[j], 16 * turn)
                    else:
                        dve.wait_ge(passes[0].sent[j], 16 * len(range(j, EXPERT_TILES, RING)))
                    dve.tensor_copy(place[j][:, :], a[:, 2 * P + 1:2 * P + 2])
                    dve.wait_ge(ps2.cent, t + 1)
                    dve.wait_ge(ps2.rstd, t + 1)
                    dve.scalar_tensor_tensor(b[:, 0:P], cent[c][:, :], rstd2[c][:, 0:1], beta_bc[:, :],
                                             ALU.mult, ALU.add).then_inc(ps2.row_done, 1)

                return centre, invert, finish

            mix(0, 0, 0, None)
            for t in range(1, RING + 1):
                mix(t, t // RING, t % RING, tail_of(t - 1, 0, t - 1, fresh=True))

            def step2(t, turn, j):
                mix(t, turn, j, tail_of(t - 1, turn - (j == 0), (j - 1) % RING))

            tiles(dve, RING + 1, step2)
            t = EXPERT_TILES - 1
            for part in tail_of(t, t // RING, t % RING):
                part()

            for n in range(STEPS):
                dve.wait_ge(silu_done, n + 1)
                dve.tensor_tensor(cols(z, n * ST, ST), cols(z, n * ST, ST), cols(s, n * ST, ST), ALU.mult)\
                    .then_inc(gated, 1)
                dve.wait_ge(gated, n + 1)
                dve.tensor_tensor(cols(z, n * ST, ST), cols(z, n * ST, ST), cols(x, n * ST, ST), ALU.add)\
                    .then_inc(out_done, 1)


def kernel(L0_attn_query, L0_attn_W_qkv, L0_attn_b_qkv, L0_attn_W_out, L0_attn_b_out, L0_attn_weight_q,
           L0_attn_weight_v, L0_ffn_gate_W, L0_ffn_gate_b, L0_ffn_W1, L0_ffn_b1, L0_ffn_W2, L0_ffn_b2,
           L0_ffn_ln_gamma, L0_ffn_ln_beta):
    import concourse.bacc as bacc
    from concourse.bass_utils import run_bass_kernel_spmd

    a = np.asarray
    wqkv, bqkv = a(L0_attn_W_qkv), a(L0_attn_b_qkv)
    arrays = {
        "query": a(L0_attn_query),
        "wq_t": wqkv[0:P].T, "wv_t": wqkv[2 * P:3 * P].T, "bq": bqkv[0:P], "bv": bqkv[2 * P:3 * P],
        "wo_t": a(L0_attn_W_out).T, "bo": a(L0_attn_b_out),
        "weight_q": a(L0_attn_weight_q).transpose(0, 2, 1).reshape(P, 3),
        "weight_v": a(L0_attn_weight_v).transpose(0, 2, 1).reshape(P, 3),
        "gate_w": a(L0_ffn_gate_W), "gate_b": a(L0_ffn_gate_b),
        "w1": a(L0_ffn_W1), "w2": a(L0_ffn_W2),
        "b12": np.concatenate([a(L0_ffn_b1), a(L0_ffn_b2)], axis=1),
        "gamma": a(L0_ffn_ln_gamma), "beta": a(L0_ffn_ln_beta),
    }
    arrays.update(consts())
    arrays = {n: np.ascontiguousarray(v) for n, v in arrays.items()}
    nc = bacc.Bacc("TRN2", target_bir_lowering=False, num_devices=1)
    io = {n: nc.dram_tensor(f"in_{n}", v.shape, mybir.dt.from_np(v.dtype), kind="ExternalInput").ap()
          for n, v in arrays.items()}
    out = nc.dram_tensor("out", (16, 256, P), F32, kind="ExternalOutput").ap()
    build(nc, io, out)
    r = run_bass_kernel_spmd(nc, [{f"in_{n}": v for n, v in arrays.items()}], core_ids=[0])
    return r.results[0]["out"]
```

```python
from contextlib import ExitStack

import numpy as np

import concourse.bass as bass
from concourse import mybir

F32 = mybir.dt.float32
BF16 = mybir.dt.bfloat16
I32 = mybir.dt.int32
U32 = mybir.dt.uint32
ALU = mybir.AluOpType
ACT = mybir.ActivationFunctionType
AX_X = mybir.AxisListType.X

P = 128
E = 8
H = 256
TOKENS = 16 * 256
TILES = TOKENS // P
GT = 8
GROUPS = TILES // GT
ST = 4
STEPS = TILES // ST
K = 2
REG = TOKENS + P
ROWS = (E + 1) * REG
EXPERT_TILES = TILES - 1 + E
RING = 8
PAIR = 2
TABLE = 48
W1_COLS = H + 2
ROW1 = P + 4
ROW2 = 2 * P + 2
NOWHERE = 1.0e6
EPS = 1e-5
C1 = 0.7071067811865476

INS = ["query", "wq_t", "wv_t", "bq", "bv", "wo_t", "bo", "weight_q", "weight_v", "gate_w", "gate_b", "w1", "w2",
       "b1", "b2", "gamma", "beta", "identity", "haar", "haar_t", "before", "tok", "pad1", "pad2", "tile_consts"]


def haar_matrix():
    c = np.float32(C1)
    m = np.zeros((P, P), np.float32)
    for k in range(P // 8):
        m[8 * k:8 * k + 8, k] = c * c * c
        m[8 * k:8 * k + 4, 16 + k] = c * c * c
        m[8 * k + 4:8 * k + 8, 16 + k] = -c * c * c
    for k in range(P // 4):
        m[4 * k:4 * k + 2, 32 + k] = c * c
        m[4 * k + 2:4 * k + 4, 32 + k] = -c * c
    for k in range(P // 2):
        m[2 * k, 64 + k] = c
        m[2 * k + 1, 64 + k] = -c
    return m


LEVELS = ((0, 16), (16, 32), (32, 64), (64, 128))


def consts():
    pad1 = np.zeros((P, ROW1), np.float32)
    pad1[:, P] = pad1[:, P + 3] = NOWHERE
    pad2 = np.zeros((P, ROW2), np.float32)
    pad2[:, 2 * P + 1] = NOWHERE
    p, t = np.arange(P), np.arange(TILES)
    line = np.concatenate([np.arange(E), np.tile(np.arange(E) * REG, K),
                           np.tril(np.ones((E, E))).ravel(), np.arange(EXPERT_TILES)]).astype(np.float32)
    return {
        "identity": np.eye(P, dtype=np.float32),
        "haar": haar_matrix(),
        "haar_t": np.ascontiguousarray(haar_matrix().T),
        "before": np.triu(np.ones((P, P), np.float32), 1),
        "tok": (t[None, :] * P + p[:, None]).astype(np.float32),
        "pad1": pad1, "pad2": pad2,
        "tile_consts": np.tile(line, (P, 1)),
    }


def build(nc, io, out):
    ctx = ExitStack()
    with ctx:
        def sb(name, shape, dt=F32):
            return ctx.enter_context(nc.sbuf_tensor(name, shape, dt))

        def sem(name):
            return ctx.enter_context(nc.semaphore(name))

        rows1_dram = nc.dram_tensor("rows1", [ROWS, ROW1], F32).ap()
        rows2_dram = nc.dram_tensor("rows2", [ROWS, ROW2], F32).ap()
        z_dram = nc.dram_tensor("z_by_token", [TOKENS, P], F32).ap()
        b2_dram = nc.dram_tensor("b2_parts", [3, E, P], BF16).ap()

        wq, wv, wo = (sb(n, [P, P]) for n in ("wq", "wv", "wo"))
        bo_bc, gamma_bc, beta_bc = (sb(n, [P, P]) for n in ("bo_bc", "gamma_bc", "beta_bc"))
        gw = sb("gw", [P, E])
        gb_bc = sb("gb_bc", [P, E])
        att_cols = sb("att_cols", [P, 8])
        att_scale = sb("att_scale", [P, 6])
        ident, haar, haar_t = (sb(n, [P, P]) for n in ("ident", "haar_sb", "haar_t_sb"))
        before_f = sb("before_f", [P, P])
        before = sb("before_sb", [P, P], BF16)
        ones = sb("ones", [P, P], BF16)
        consts_sb = sb("consts_sb", [P, E + K * E + E * E + EXPERT_TILES])
        iota_e = consts_sb[:, 0:E]
        region = consts_sb[:, E:E + K * E]
        tril = consts_sb[:, E + K * E:E + K * E + E * E]
        iota_t = consts_sb[:, E + K * E + E * E:]
        pad1, pad2 = sb("pad1_sb", [P, ROW1]), sb("pad2_sb", [P, ROW2])
        eps_col = sb("eps_col", [P, 1])
        w2 = sb("w2_sb", [P, E * 2 * P])
        w1_all = sb("w1_all", [P, E * W1_COLS])
        w1 = [sb(f"w1_{j}", [P, W1_COLS]) for j in range(2 * PAIR)]
        b2_row = sb("b2_row", [E, P])
        b2_rest = sb("b2_rest", [E, 2, P])
        b2_part = sb("b2_part", [E, 3, P], BF16)
        b2 = sb("b2_sb", [P, E * P], BF16)

        x = sb("x", [P, TILES * P])
        s = sb("s", [P, TILES * P])
        tok = sb("tok_sb", [P, TILES])

        rows = [sb(f"rows_{b}", [P, GT, ROW1]) for b in range(2)]
        slot1 = [sb(f"slot1_{b}", [P, GT], I32) for b in range(2)]
        stats = sb("stats", [P, GT, 6])
        moments = sb("moments", [P, GT, 2])
        var = sb("var", [P, GT])
        half_bits = sb("half_bits", [P, GT], I32)
        rstd = sb("rstd", [P, GT])
        newton = sb("newton", [P, GT])
        xt = [sb(f"xt_{u}", [P, ST * P]) for u in range(2)]
        hx = [sb(f"hx_{u}", [P, ST * P]) for u in range(4)]
        logits = sb("logits", [P, GT, E])
        top = sb("top", [P, GT, 8])
        top_at = sb("top_at", [P, GT, 8], U32)
        onehot = sb("onehot", [P, GT, K, E], BF16)
        shifted = sb("shifted", [P, GT, E + 1])
        expd = sb("expd", [P, GT, E + 1])
        total = sb("total", [P, GT])
        places = sb("places", [P, GT, K * E])
        chosen = sb("chosen", [P, GT, K, E])
        slots = sb("slots", [P, GT, K])
        carry = sb("carry", [P, K * E])
        qw = [sb(f"qw_{b}", [P, ST * P]) for b in range(2)]
        prod = [sb(f"prod_{b}", [P, ST * P]) for b in range(2)]
        y_sb = [sb(f"y_sb_{b}", [P, ST * P]) for b in range(2)]

        counts = sb("counts", [1, K * E])
        counts_i = sb("counts_i", [1, K * E], I32)
        n_tiles = sb("n_tiles", [1, K * E])
        tri = sb("tri", [1, K, E, E])
        ends = sb("ends", [1, K, E])
        past = sb("past", [1, K, EXPERT_TILES, E])
        past_n = sb("past_n", [1, K, EXPERT_TILES, E])
        t_expert = sb("t_expert", [1, K, EXPERT_TILES])
        t_start = sb("t_start", [1, K, EXPERT_TILES])
        t_row = sb("t_row", [1, K, EXPERT_TILES])
        table_row = sb("table_row", [1, K * TABLE], I32)
        table_expert = sb("table_expert", [1, K * TABLE], I32)
        pad_at = sb("pad_at", [1, K * (E + 1)], I32)

        row_in = [sb(f"row_in_{j}", [P, ROW2]) for j in range(RING)]
        row_out = [sb(f"row_out_{j}", [P, ROW2]) for j in range(RING)]
        place = [sb(f"place_{j}", [P, 1], I32) for j in range(RING)]
        et = [sb(f"et_{b}", [P, P]) for b in range(2)]
        hid = [sb(f"hid_{b}", [P, 2 * P]) for b in range(2)]
        res = [sb(f"res_{b}", [P, P]) for b in range(2)]
        cent = [sb(f"cent_{b}", [P, P]) for b in range(2)]
        st2 = [sb(f"st2_{b}", [P, 6]) for b in range(2)]
        mv2 = [sb(f"mv2_{b}", [P, 2]) for b in range(2)]
        std2 = [sb(f"std2_{b}", [P, 1]) for b in range(2)]
        rstd2 = [sb(f"rstd2_{b}", [P, 1]) for b in range(2)]
        z = sb("z", [P, TILES * P])

        bank = [ctx.enter_context(nc.psum_tensor(f"bank{i}", [P, 512], F32)) for i in range(8)]
        ps_x, ps_lg, ps_rk, ps_q, ps_v, ps_y, ps_s = bank[0:2], bank[2], bank[3], bank[4], bank[5], bank[6], bank[7]
        ps_t, ps_h, ps_o = bank[0:2], bank[2:4], bank[4:6]

        x_in = [sem(f"x_in_{g}") for g in range(GROUPS)]
        const_in = sem("const_in")
        att_in = sem("att_in")
        late_in = sem("late_in")
        b_in = sem("b_in")
        zeroed = sem("zeroed")
        set_up = sem("set_up")
        b_parts = sem("b_parts")
        b_stored = sem("b_stored")
        b_loaded = sem("b_loaded")
        stats_done = sem("stats_done")
        moments_done = sem("moments_done")
        rstd_step = sem("rstd_step")
        xn_done = sem("xn_done")
        xt_psum = sem("xt_psum")
        xt_sbuf = sem("xt_sbuf")
        logits_psum = sem("logits_psum")
        logits_sbuf = sem("logits_sbuf")
        top_done = sem("top_done")
        top_at_done = sem("top_at_done")
        onehot_done = sem("onehot_done")
        shifted_done = sem("shifted_done")
        exp_done = sem("exp_done")
        total_done = sem("total_done")
        weight1_done = sem("weight1_done")
        rank_psum = sem("rank_psum")
        places_done = sem("places_done")
        carry_done = sem("carry_done")
        chosen_done = sem("chosen_done")
        slots_done = sem("slots_done")
        meta_done = sem("meta_done")
        sent = [[sem(f"sent_{b}_{t}") for t in range(GT)] for b in range(2)]
        hx_psum = sem("hx_psum")
        hx_sbuf = sem("hx_sbuf")
        q_psum = sem("q_psum")
        v_psum = sem("v_psum")
        qw_done = sem("qw_done")
        prod_done = sem("prod_done")
        y_psum = sem("y_psum")
        y_sbuf = sem("y_sbuf")
        s_psum = sem("s_psum")
        s_sbuf = sem("s_sbuf")
        table_step = sem("table_step")
        table_done = sem("table_done")
        pads1 = sem("pads1")
        pads2 = sem("pads2")

        class Pass:
            def __init__(self, k):
                self.k = k
                self.rows_in = [sem(f"p{k}_rows_in_{j}") for j in range(RING)]
                self.sent = [sem(f"p{k}_sent_{j}") for j in range(RING)]
                self.et_psum = sem(f"p{k}_et_psum")
                self.et_sbuf = sem(f"p{k}_et_sbuf")
                self.hid_psum = sem(f"p{k}_hid_psum")
                self.hid_sbuf = sem(f"p{k}_hid_sbuf")
                self.o_psum = sem(f"p{k}_o_psum")
                self.o_read = sem(f"p{k}_o_read")
                self.row_done = sem(f"p{k}_row_done")
                self.scattering = sem(f"p{k}_scattering")
                self.stats = sem(f"p{k}_stats")
                self.moments = sem(f"p{k}_moments")
                self.std = sem(f"p{k}_std")
                self.rstd = sem(f"p{k}_rstd")
                self.cent = sem(f"p{k}_cent")

        passes = [Pass(0), Pass(1)]
        z_in = [sem(f"z_in_{n}") for n in range(STEPS)]
        silu_done = sem("silu_done")
        gated = sem("gated")
        out_done = sem("out_done")
        out_stored = sem("out_stored")

        query_v = io["query"].rearrange("b l d -> (b l) d").rearrange("(t p) d -> p t d", p=P)
        out_v = out.rearrange("b l d -> (b l) d").rearrange("(t p) d -> p t d", p=P)
        z_v = z_dram.rearrange("(t p) d -> p t d", p=P)

        def cols(ap, t, n=1):
            return ap[:, t * P:(t + n) * P]

        def by_tile(ap, n):
            return ap.rearrange("p (t c) -> p t c", t=n)

        def entries(eng, table, k, first, n):
            top = (E - 1) if table is table_expert else E * REG
            _, values = nc.values_load_multi_w_load_instructions(
                table[0:1, bass.ds(first + k * TABLE, n)], engines=[eng.engine], min_val=0, max_val=top,
                skip_runtime_bounds_check_because="VectorE clamps every entry to this range")
            return values

        def tiles(eng, first, end, step, table=None, k=0, ahead=0):
            def turn(t0, i, n):
                ent = entries(eng, table, k, t0 + ahead, n) if table is not None else [None] * n
                for j in range(n):
                    step(t0 + j, i + (first + j) // RING, (first + j) % RING, ent[j])

            loops = (end - first) // RING
            with eng.Fori(0, loops) as i:
                turn(i * RING + first, i, RING)
            rest = first + loops * RING
            if rest < end:
                turn(rest, loops, end - rest)

        block = ctx.enter_context(nc.Block())

        @block.sync
        def _(sp):
            sp.dma_start(by_tile(cols(x, 0, GT), GT), query_v[:, 0:GT, :]).then_inc(x_in[0], 16)
            first = [(ident[:, :], io["identity"]), (gw[:, :], io["gate_w"]),
                     (gb_bc[:, :], io["gate_b"].rearrange("(a n) -> a n", a=1).to_broadcast([P, E])),
                     (haar[:, :], io["haar"]), (before_f[:, :], io["before"]), (consts_sb[:, :], io["tile_consts"]),
                     (tok[:, :], io["tok"])]
            for dst, src in first:
                sp.dma_start(dst, src).then_inc(const_in, 16)
            for g in range(1, GROUPS):
                sp.dma_start(by_tile(cols(x, g * GT, GT), GT), query_v[:, g * GT:(g + 1) * GT, :])\
                    .then_inc(x_in[g], 16)
            sp.wait_ge(b_parts, 5)
            for k in range(3):
                sp.dma_start(b2_dram[k], b2_part[:, k, :]).then_inc(b_stored, 16)
            sp.wait_ge(b_stored, 48)
            sp.wait_ge(zeroed, 1)
            sp.dma_start(b2[0:3, :], b2_dram.rearrange("k e n -> k (e n)")).then_inc(b_loaded, 16)
            sp.wait_ge(table_done, 1)
            sp.wait_ge(late_in, 16 * 7)
            with sp.Fori(0, E + 1) as e:
                at = sp.value_load(pad_at[0:1, bass.ds(e, 1)], min_val=0, max_val=E * REG)
                sp.dma_start(rows1_dram[bass.ds(at, P), :], pad1[:, :]).then_inc(pads1, 16)

            for ps in passes:
                src, width = (rows1_dram, ROW1) if ps.k == 0 else (rows2_dram, ROW2)

                def load_rows(t, turn, j, row):
                    sp.dma_start(row_in[j][:, 0:width], src[bass.ds(row, P), :]).then_inc(ps.rows_in[j], 16)

                if ps.k == 0:
                    for g in range(GROUPS - 2, GROUPS):
                        for t in range(GT):
                            sp.wait_ge(sent[g % 2][t], 16 * (g // 2 + 1))
                    sp.wait_ge(pads1, 16 * (E + 1))
                else:
                    sp.wait_ge(table_done, 2)
                    for j in range(RING):
                        sp.wait_ge(passes[0].sent[j], 16 * len(range(j, EXPERT_TILES, RING)))
                    sp.wait_ge(pads2, 16 * (E + 1))
                    sp.wait_ge(passes[0].row_done, EXPERT_TILES)
                for t, row in enumerate(entries(sp, table_row, ps.k, 0, RING)):
                    load_rows(t, 0, t, row)

                def step(t, turn, j, row):
                    sp.wait_ge(ps.row_done, t - RING + 1)
                    load_rows(t, turn, j, row)

                tiles(sp, RING, EXPERT_TILES, step, table_row, ps.k)

            for j in range(RING):
                sp.wait_ge(passes[1].sent[j], 16 * len(range(j, EXPERT_TILES, RING)))
            for n in range(STEPS):
                sp.dma_start(by_tile(cols(z, n * ST, ST), ST), z_v[:, n * ST:(n + 1) * ST, :]).then_inc(z_in[n], 16)
            for n in range(STEPS):
                sp.wait_ge(out_done, n + 1)
                sp.dma_start(out_v[:, n * ST:(n + 1) * ST, :], by_tile(cols(z, n * ST, ST), ST))\
                    .then_inc(out_stored, 16)
            sp.wait_ge(out_stored, 16 * STEPS)

        @block.gpsimd
        def _(pool):
            pool.memset(b2[:, :].bitcast(I32), 0).then_inc(zeroed, 1)
            pool.memset(ones[:, :], 1.0).then_inc(zeroed, 1)
            pool.memset(eps_col[:, :], EPS).then_inc(zeroed, 1)
            for g in range(GROUPS):
                pool.wait_ge(meta_done, g + 1)
                for t in range(GT):
                    pool.indirect_dma_start(
                        out=rows1_dram[:, :], out_offset=bass.IndirectOffsetOnAxis(ap=slot1[g % 2][:, t:t + 1], axis=0),
                        in_=rows[g % 2][:, t, :], in_offset=None,
                        bounds_check=ROWS - 1, oob_is_err=False).then_inc(sent[g % 2][t], 16)
            for ps in passes:
                dst, width, last = (rows2_dram, ROW2, ROWS - 1) if ps.k == 0 else (z_dram, P, TOKENS - 1)

                def step(t, turn, j, _):
                    pool.wait_ge(ps.row_done, t + 1)
                    pool.sem_inc(ps.scattering, 1)
                    pool.indirect_dma_start(
                        out=dst[:, :], out_offset=bass.IndirectOffsetOnAxis(ap=place[j][:, 0:1], axis=0),
                        in_=row_out[j][:, 0:width], in_offset=None,
                        bounds_check=last, oob_is_err=False).then_inc(ps.sent[j], 16)

                tiles(pool, 0, EXPERT_TILES, step)

        @block.tensor
        def _(pe):
            def transposes(g):
                for u in range(2):
                    if g:
                        pe.wait_ge(hx_sbuf, 2 * (g - 1) + u + 1)
                    for t in range(ST):
                        pe.wait_ge(xn_done, GT * g + ST * u + t + 1)
                        mm = pe.transpose(cols(ps_x[u], t), rows[g % 2][:, ST * u + t, 0:P], ident[:, :])
                    mm.then_inc(xt_psum, 1)

            def gate(g):
                if g:
                    pe.wait_ge(logits_sbuf, g)
                for u in range(2):
                    pe.wait_ge(xt_sbuf, 2 * g + u + 1)
                    for t in range(ST):
                        at = (ST * u + t) * E
                        mm = pe.matmul(ps_lg[:, at:at + E], cols(xt[u], t), gw[:, :], start=True, stop=True)
                mm.then_inc(logits_psum, 1)

            def haar_coefs(g):
                for u in range(2):
                    pe.wait_ge(xt_sbuf, 2 * g + u + 1)
                    for t in range(ST):
                        mm = pe.matmul(cols(ps_x[u], t), rows[g % 2][:, ST * u + t, 0:P], haar[:, :],
                                       start=True, stop=True)
                    mm.then_inc(hx_psum, 1)

            def ranks(g):
                pe.wait_ge(onehot_done, g + 1)
                if g:
                    pe.wait_ge(carry_done, g)
                    pe.wait_ge(places_done, g)
                oh = onehot[:, :, :, :].rearrange("p t k e -> p t (k e)")
                n = K * E
                for t in range(GT):
                    pe.matmul(ps_rk[:, GT * n:GT * n + n], ones[:, :], oh[:, t, :], start=(t == 0), stop=(t == GT - 1))
                mm = pe.matmul(ps_rk[:, 0:GT * n], before[:, :], oh.rearrange("p t n -> p (t n)"),
                               start=True, stop=False, skip_group_check=True)
                for t in range(GT - 1):
                    later = GT - 1 - t
                    mm = pe.matmul(ps_rk[:, (t + 1) * n:GT * n].rearrange("p (t n) -> p t n", t=later), ones[:, :],
                                   oh[:, t:t + 1, :].to_broadcast([P, later, n]), start=False,
                                   stop=(t == GT - 2), skip_group_check=True)
                mm.then_inc(rank_psum, 1)

            def q_of(n):
                if n:
                    pe.wait_ge(qw_done, n)
                pe.wait_ge(hx_sbuf, n + 1)
                pe.matmul(ps_q[:, :], wq[:, :], hx[n % 4][:, :], start=True, stop=True).then_inc(q_psum, 1)

            def v_of(n):
                if n:
                    pe.wait_ge(prod_done, n)
                pe.matmul(ps_v[:, :], wv[:, :], hx[n % 4][:, :], start=True, stop=True).then_inc(v_psum, 1)

            def y_of(n):
                pe.wait_ge(prod_done, n + 1)
                if n:
                    pe.wait_ge(y_sbuf, n)
                for t in range(ST):
                    mm = pe.matmul(cols(ps_y, t), cols(prod[n % 2], t), wo[:, :], start=True, stop=True)
                mm.then_inc(y_psum, 1)

            def s_of(n):
                pe.wait_ge(y_sbuf, n + 1)
                if n:
                    pe.wait_ge(s_sbuf, n)
                pe.matmul(ps_s[:, :], haar_t[:, :], y_sb[n % 2][:, :], start=True, stop=True).then_inc(s_psum, 1)

            def attention(n):
                if n < STEPS:
                    q_of(n)
                if n:
                    y_of(n - 1)
                if n < STEPS:
                    v_of(n)
                if n:
                    s_of(n - 1)

            pe.wait_ge(const_in, 16 * 7)
            pe.wait_ge(set_up, 1)
            for g in range(GROUPS):
                transposes(g)
                gate(g)
                haar_coefs(g)
                if g == 0:
                    pe.wait_ge(zeroed, 3)
                    ranks(g)
                    pe.wait_ge(att_in, 16 * 8)
                else:
                    attention(2 * g - 2)
                    ranks(g)
                    attention(2 * g - 1)
            attention(STEPS - 2)
            attention(STEPS - 1)
            attention(STEPS)

            pe.wait_ge(b_loaded, 16)
            pe.wait_ge(late_in, 16 * 7)
            pe.wait_ge(s_sbuf, STEPS)
            for ps in passes:
                def turn_rows(turn, j):
                    pe.wait_ge(ps.rows_in[j], 16 * (turn + 1))
                    pe.transpose(ps_t[j % 2][:, 0:P], row_in[j][:, 0:P], ident[:, :]).then_inc(ps.et_psum, 1)

                def layer1(t, j):
                    pe.wait_ge(ps.et_sbuf, t + 1)
                    for c in range(2):
                        mm = pe.matmul(cols(ps_h[j % 2], c), cols(w1[j % 4], c), et[j % 2][:, :], start=True, stop=True)
                    mm.then_inc(ps.hid_psum, 1)

                def layer2(t, j, expert, fresh=False):
                    pe.wait_ge(ps.hid_sbuf, t + 1)
                    if not fresh:
                        pe.wait_ge(ps.o_read, t - 1)
                    o = ps_o[j % 2][:, 0:P]
                    for c in range(2):
                        pe.matmul(o, cols(hid[j % 2], c), w2[:, bass.ds(expert * 2 * P + c * P, P)],
                                  start=(c == 0), stop=False)
                    pe.matmul(o, ones[:, :], b2[:, bass.ds(expert * P, P)],
                              start=False, stop=True).then_inc(ps.o_psum, 1)

                pe.wait_ge(table_done, ps.k + 1)
                first = entries(pe, table_expert, ps.k, 0, 4)
                turn_rows(0, 0)
                turn_rows(0, 1)
                layer1(0, 0)
                turn_rows(0, 2)
                for t in range(1, 3):
                    layer1(t, t)
                    turn_rows(0, t + 2)
                    layer2(t - 1, t - 1, first[t - 1], fresh=True)

                def step(t, turn, j, expert, ahead=True):
                    layer1(t, j)
                    if ahead:
                        turn_rows(turn + (j + 2) // RING, (j + 2) % RING)
                    layer2(t - 1, (j - 1) % RING, expert)

                last = EXPERT_TILES - 2 - (EXPERT_TILES - 2 - 3) % RING
                tiles(pe, 3, last, step, table_expert, ps.k, ahead=-1)
                left = entries(pe, table_expert, ps.k, last - 1, EXPERT_TILES - last + 1)
                for n, t in enumerate(range(last, EXPERT_TILES)):
                    step(t, t // RING, t % RING, left[n], ahead=t + 2 < EXPERT_TILES)
                t = EXPERT_TILES - 1
                layer2(t, t % RING, left[-1])

        @block.scalar
        def _(act):
            loads = [(wq[:, :], io["wq_t"]), (wv[:, :], io["wv_t"]), (wo[:, :], io["wo_t"]),
                     (haar_t[:, :], io["haar_t"]),
                     (att_cols[:, 0:1], io["bq"].rearrange("(p a) -> p a", a=1)),
                     (att_cols[:, 1:2], io["bv"].rearrange("(p a) -> p a", a=1)),
                     (att_cols[:, 2:5], io["weight_q"]), (att_cols[:, 5:8], io["weight_v"])]
            for dst, src in loads:
                act.dma_start(dst, src).then_inc(att_in, 16)
            act.dma_start(b2_row[:, :], io["b2"]).then_inc(b_in, 16)
            act.dma_start(bo_bc[:, :], io["bo"].rearrange("(a n) -> a n", a=1).to_broadcast([P, P])).then_inc(b_in, 16)

            def xt_copy(g):
                for u in range(2):
                    act.wait_ge(xt_psum, 2 * g + u + 1)
                    if g:
                        act.wait_ge(logits_psum, g)
                    act.activation(xt[u][:, :], ps_x[u][:, :], ACT.Copy).then_inc(xt_sbuf, 1)

            def hx_copy(g):
                for u in range(2):
                    n = 2 * g + u
                    act.wait_ge(hx_psum, n + 1)
                    if n >= 4:
                        act.wait_ge(v_psum, n - 3)
                    act.activation(hx[n % 4][:, :], ps_x[u][:, :], ACT.Copy).then_inc(hx_sbuf, 1)

            def exps(g):
                act.wait_ge(shifted_done, g + 1)
                if g:
                    act.wait_ge(weight1_done, 2 * g)
                act.activation(expd[:, :, :], shifted[:, :, :], ACT.Exp).then_inc(exp_done, 1)

            def qw_of(n):
                act.wait_ge(q_psum, n + 1)
                if n >= 2:
                    act.wait_ge(prod_done, n - 1)
                src, dst = by_tile(ps_q[:, :], ST), by_tile(qw[n % 2][:, :], ST)
                for k, (a, b) in enumerate(LEVELS):
                    if k == 0:
                        ins = act.activation(dst[:, :, a:b], src[:, :, a:b], ACT.Identity,
                                             bias=att_scale[:, 0:1], scale=att_scale[:, 2:3])
                    elif k < 3:
                        ins = act.activation(dst[:, :, a:b], src[:, :, a:b], ACT.Copy, scale=att_scale[:, 2 + k:3 + k])
                    else:
                        ins = act.activation(dst[:, :, a:b], src[:, :, a:b], ACT.Copy)
                ins.then_inc(qw_done, 1)

            def y_copy(n):
                act.wait_ge(y_psum, n + 1)
                if n >= 2:
                    act.wait_ge(s_psum, n - 1)
                act.activation(y_sb[n % 2][:, :], ps_y[:, :], ACT.Copy).then_inc(y_sbuf, 1)

            def attention(n):
                if n < STEPS:
                    qw_of(n)
                if n:
                    y_copy(n - 1)

            for g in range(GROUPS):
                xt_copy(g)
                hx_copy(g)
                exps(g)
                if g == 0:
                    late = [(w2[:, :].rearrange("p (e c d) -> p e c d", e=E, c=2),
                             io["w2"].rearrange("e (c p) d -> p e c d", p=P)),
                            (w1_all[:, :].rearrange("p (e h) -> p e h", e=E)[:, :, 0:H],
                             io["w1"].rearrange("e p h -> p e h")),
                            (w1_all[:, :].rearrange("p (e h) -> p e h", e=E)[:, :, H:W1_COLS], io["b1"]),
                            (pad1[:, :], io["pad1"]), (pad2[:, :], io["pad2"]),
                            (gamma_bc[:, :], io["gamma"].rearrange("(a n) -> a n", a=1).to_broadcast([P, P])),
                            (beta_bc[:, :], io["beta"].rearrange("(a n) -> a n", a=1).to_broadcast([P, P]))]
                    for dst, src in late:
                        act.dma_start(dst, src).then_inc(late_in, 16)
                    act.wait_ge(set_up, 4)
                else:
                    attention(2 * g - 2)
                    attention(2 * g - 1)
            attention(STEPS - 2)
            act.wait_ge(table_done, 1)
            act.wait_ge(late_in, 16 * 7)
            with act.Fori(0, E + 1) as e:
                at = act.value_load(pad_at[0:1, bass.ds(e + E + 1, 1)], min_val=0, max_val=E * REG)
                act.dma_start(rows2_dram[bass.ds(at, P), :], pad2[:, :]).then_inc(pads2, 16)
            attention(STEPS - 1)
            attention(STEPS)

            for ps in passes:
                def turned(t, j, expert):
                    act.activation(w1[j % 4][:, :], w1_all[:, bass.ds(expert * W1_COLS, W1_COLS)], ACT.Copy)
                    act.wait_ge(ps.et_psum, t + 1)
                    act.activation(et[j % 2][:, :], ps_t[j % 2][:, 0:P], ACT.Copy).then_inc(ps.et_sbuf, 1)

                def relu(t, j, fresh=False):
                    act.wait_ge(ps.hid_psum, t + 1)
                    if not fresh:
                        act.wait_ge(ps.o_psum, t - 1)
                    for c in range(2):
                        ins = act.activation(cols(hid[j % 2], c), cols(ps_h[j % 2], c), ACT.Relu,
                                             bias=w1[j % 4][:, H + c:H + c + 1])
                    ins.then_inc(ps.hid_sbuf, 1)

                def deviation(t, j, fresh=False):
                    act.wait_ge(ps.moments, t + 1)
                    if not fresh:
                        act.wait_ge(ps.rstd, t - 1)
                    act.activation(std2[j % 2][:, :], mv2[j % 2][:, 1:2], ACT.Sqrt, bias=eps_col[:, 0:1])\
                        .then_inc(ps.std, 1)

                if ps.k == 1:
                    act.activation(std2[0][:, :], eps_col[:, 0:1], ACT.Sqrt)
                first = entries(act, table_expert, ps.k, 0, 6)
                turned(0, 0, first[0])
                turned(1, 1, first[1])
                for t in range(4):
                    relu(t, t, fresh=t < 2)
                    turned(t + 2, t + 2, first[t + 2])
                    if ps.k == 1 and t >= 2:
                        deviation(t - 2, t - 2, fresh=True)

                def step(t, turn, j, expert):
                    relu(t, j)
                    if expert is not None:
                        turned(t + 2, (j + 2) % RING, expert)
                    if ps.k == 1:
                        deviation(t - 2, (j - 2) % RING)

                tiles(act, 4, EXPERT_TILES - 2, step, table_expert, ps.k, ahead=2)
                for t in range(EXPERT_TILES - 2, EXPERT_TILES):
                    step(t, t // RING, t % RING, None)
                if ps.k == 1:
                    for t in range(EXPERT_TILES - 2, EXPERT_TILES):
                        deviation(t, t % RING)

            for n in range(STEPS):
                act.wait_ge(z_in[n], 16)
                act.activation(cols(z, n * ST, ST), cols(z, n * ST, ST), ACT.Silu).then_inc(silu_done, 1)

        @block.vector
        def _(dve):
            rstd_steps = [0]

            def rstd_next(ins):
                rstd_steps[0] += 1
                ins.then_inc(rstd_step, 1)
                dve.wait_ge(rstd_step, rstd_steps[0])

            def layer_norm(g):
                dve.wait_ge(x_in[g], 16)
                for t in range(GT):
                    ins = dve.bn_stats(stats[:, t, :], cols(x, GT * g + t))
                ins.then_inc(stats_done, 1)
                dve.wait_ge(stats_done, g + 1)
                for t in range(GT):
                    ins = dve.bn_aggr(moments[:, t, :], stats[:, t, :])
                ins.then_inc(moments_done, 1)
                dve.wait_ge(moments_done, g + 1)
                rstd_next(dve.tensor_scalar(var[:, :], moments[:, :, 1], EPS, None, ALU.add))
                rstd_next(dve.tensor_scalar(half_bits[:, :], var[:, :].bitcast(I32), 1, None,
                                            ALU.logical_shift_right))
                rstd_next(dve.tensor_scalar(rstd[:, :].bitcast(I32), half_bits[:, :], -1.0, float(0x5f3759df),
                                            ALU.mult, ALU.add))
                for _ in range(3):
                    rstd_next(dve.tensor_tensor(newton[:, :], rstd[:, :], rstd[:, :], ALU.mult))
                    rstd_next(dve.scalar_tensor_tensor(newton[:, :], newton[:, :], -0.5, var[:, :],
                                                       ALU.mult, ALU.mult))
                    rstd_next(dve.scalar_tensor_tensor(rstd[:, :], newton[:, :], 1.5, rstd[:, :],
                                                       ALU.add, ALU.mult))
                for t in range(GT):
                    if g >= 2:
                        dve.wait_ge(sent[g % 2][t], 16 * (g // 2))
                        dve.wait_ge(hx_psum, 2 * g - 2)
                    dve.tensor_scalar(rows[g % 2][:, t, 0:P], cols(x, GT * g + t), moments[:, t, 0:1],
                                      rstd[:, t:t + 1], ALU.subtract, ALU.mult).then_inc(xn_done, 1)

            def route(g):
                dve.wait_ge(logits_psum, g + 1)
                dve.tensor_tensor(logits[:, :, :], ps_lg[:, 0:GT * E].rearrange("p (t e) -> p t e", t=GT),
                                  gb_bc[:, None, :].to_broadcast([P, GT, E]), ALU.add).then_inc(logits_sbuf, 1)
                dve.wait_ge(logits_sbuf, g + 1)
                for t in range(GT):
                    ins = dve.max(top[:, t, :], logits[:, t, :])
                ins.then_inc(top_done, 1)
                dve.wait_ge(top_done, g + 1)
                for t in range(GT):
                    ins = dve.max_index(top_at[:, t, :], top[:, t, :], logits[:, t, :])
                ins.then_inc(top_at_done, 1)
                dve.tensor_tensor(shifted[:, :, 0:E], logits[:, :, :], top[:, :, 0:1].to_broadcast([P, GT, E]),
                                  ALU.subtract)
                dve.tensor_tensor(shifted[:, :, E], top[:, :, 1], top[:, :, 0], ALU.subtract)\
                    .then_inc(shifted_done, 1)
                dve.wait_ge(top_at_done, g + 1)
                if g:
                    dve.wait_ge(rank_psum, g)
                dve.tensor_tensor(onehot[:, :, :, :],
                                  iota_e[:, None, None, :].to_broadcast([P, GT, K, E]),
                                  top_at[:, :, 0:K][:, :, :, None].to_broadcast([P, GT, K, E]), ALU.is_equal)\
                    .then_inc(onehot_done, 1)

            def weights(g):
                dve.wait_ge(exp_done, g + 1)
                dve.tensor_reduce(total[:, :], expd[:, :, 0:E], AX_X, ALU.add).then_inc(total_done, 1)
                dve.wait_ge(total_done, g + 1)
                dve.reciprocal(rows[g % 2][:, :, P + 1], total[:, :]).then_inc(weight1_done, 1)
                dve.wait_ge(weight1_done, 2 * g + 1)
                dve.tensor_tensor(rows[g % 2][:, :, P + 2], expd[:, :, E], rows[g % 2][:, :, P + 1], ALU.mult)\
                    .then_inc(weight1_done, 1)

            def place_rows(g):
                dve.wait_ge(rank_psum, g + 1)
                n = K * E
                dve.tensor_tensor(places[:, :, :], ps_rk[:, 0:GT * n].rearrange("p (t n) -> p t n", t=GT),
                                  carry[:, None, :].to_broadcast([P, GT, n]), ALU.add).then_inc(places_done, 1)
                dve.wait_ge(places_done, g + 1)
                dve.tensor_tensor(carry[:, :], carry[:, :], ps_rk[:, GT * n:GT * n + n], ALU.add)\
                    .then_inc(carry_done, 1)
                dve.tensor_tensor(chosen[:, :, :, :], places[:, :, :].rearrange("p t (k e) -> p t k e", k=K),
                                  onehot[:, :, :, :], ALU.mult).then_inc(chosen_done, 1)
                dve.wait_ge(chosen_done, g + 1)
                dve.tensor_reduce(slots[:, :, :], chosen[:, :, :, :], AX_X, ALU.add).then_inc(slots_done, 1)
                dve.tensor_copy(rows[g % 2][:, :, P + 3], tok[:, g * GT:(g + 1) * GT])
                dve.wait_ge(slots_done, g + 1)
                dve.tensor_copy(rows[g % 2][:, :, P], slots[:, :, 1])
                dve.tensor_copy(slot1[g % 2][:, :], slots[:, :, 0]).then_inc(meta_done, 1)

            def attention(n):
                if n < STEPS:
                    dve.wait_ge(v_psum, n + 1)
                    dve.wait_ge(qw_done, n + 1)
                    if n >= 2:
                        dve.wait_ge(y_psum, n - 1)
                    v, q, o = (by_tile(a[:, :], ST) for a in (ps_v, qw[n % 2], prod[n % 2]))
                    b = LEVELS[0][1]
                    dve.scalar_tensor_tensor(o[:, :, 0:b], v[:, :, 0:b], att_scale[:, 1:2], q[:, :, 0:b],
                                             ALU.add, ALU.mult)
                    dve.tensor_tensor(o[:, :, b:P], v[:, :, b:P], q[:, :, b:P], ALU.mult).then_inc(prod_done, 1)
                if n:
                    dve.wait_ge(s_psum, n)
                    dve.tensor_tensor(by_tile(cols(s, (n - 1) * ST, ST), ST), by_tile(ps_s[:, :], ST),
                                      bo_bc[:, None, :].to_broadcast([P, ST, P]), ALU.add).then_inc(s_sbuf, 1)

            table_steps = [0]

            def table_next(ins):
                table_steps[0] += 1
                ins.then_inc(table_step, 1)
                dve.wait_ge(table_step, table_steps[0])

            def tile_counts():
                dve.wait_ge(carry_done, GROUPS)
                dve.tensor_copy(pad_at[0:1, :].rearrange("a (k e) -> a k e", k=K)[:, :, 0:E],
                                carry[0:1, :].rearrange("a (k e) -> a k e", k=K))
                dve.memset(pad_at[0:1, :].rearrange("a (k e) -> a k e", k=K)[:, :, E], E * REG)
                table_next(dve.tensor_tensor(counts[:, :], carry[0:1, :], region[0:1, :], ALU.subtract))
                table_next(dve.tensor_scalar(counts_i[:, :], counts[:, :], float(P - 1), None, ALU.add))
                table_next(dve.tensor_scalar(counts_i[:, :], counts_i[:, :], 7, None, ALU.logical_shift_right))
                table_next(dve.tensor_copy(n_tiles[:, :], counts_i[:, :]))
                for k in range(K):
                    nt = n_tiles[:, k * E:(k + 1) * E]
                    table_next(dve.tensor_tensor(tri[:, k, :, :], tril[0:1, :].rearrange("a (i j) -> a i j", i=E),
                                                 nt[:, None, :].to_broadcast([1, E, E]), ALU.mult))
                    table_next(dve.tensor_reduce(ends[:, k, :], tri[:, k, :, :], AX_X, ALU.add))

            def tile_table(k):
                shape = [1, EXPERT_TILES, E]
                nt = n_tiles[:, k * E:(k + 1) * E]
                it = iota_t[0:1, :]
                table_next(dve.tensor_tensor(past[:, k], it[:, :, None].to_broadcast(shape),
                                             ends[:, k:k + 1, :].to_broadcast(shape), ALU.is_ge))
                dve.tensor_reduce(t_expert[:, k, :], past[:, k], AX_X, ALU.add)
                table_next(dve.tensor_tensor(past_n[:, k], past[:, k], nt[:, None, :].to_broadcast(shape), ALU.mult))
                table_next(dve.tensor_reduce(t_start[:, k, :], past_n[:, k], AX_X, ALU.add))
                table_next(dve.scalar_tensor_tensor(t_row[:, k, :], t_expert[:, k, :], float(REG // P), it,
                                                    ALU.mult, ALU.add))
                table_next(dve.tensor_tensor(t_row[:, k, :], t_row[:, k, :], t_start[:, k, :], ALU.subtract))
                at = slice(k * TABLE, k * TABLE + EXPERT_TILES)
                dve.tensor_scalar(table_row[:, at], t_row[:, k, :], float(P), float(E * REG), ALU.mult, ALU.min)
                dve.tensor_scalar(table_expert[:, at], t_expert[:, k, :], float(E - 1), None, ALU.min)\
                    .then_inc(table_done, 1)

            dve.wait_ge(const_in, 16 * 7)
            dve.tensor_copy(before[:, :], before_f[:, :])
            dve.tensor_copy(carry[:, :], region).then_inc(set_up, 1)
            layer_norm(0)
            route(0)
            dve.wait_ge(att_in, 16 * 8)
            dve.tensor_tensor(att_scale[:, 2:5], att_cols[:, 2:5], att_cols[:, 5:8], ALU.mult).then_inc(set_up, 1)
            dve.tensor_scalar(att_scale[:, 1:2], att_cols[:, 1:2], 8 * C1 ** 3, None, ALU.mult).then_inc(set_up, 1)
            weights(0)
            dve.wait_ge(set_up, 3)
            dve.scalar_tensor_tensor(att_scale[:, 0:1], att_cols[:, 0:1], 8 * C1 ** 3, att_scale[:, 2:3],
                                     ALU.mult, ALU.mult).then_inc(set_up, 1)
            place_rows(0)
            dve.wait_ge(b_in, 32)
            dve.tensor_copy(b2_part[:, 0, :], b2_row[:, :]).then_inc(b_parts, 1)
            dve.wait_ge(b_parts, 1)
            dve.tensor_tensor(b2_rest[:, 0, :], b2_row[:, :], b2_part[:, 0, :], ALU.subtract).then_inc(b_parts, 1)
            dve.wait_ge(b_parts, 2)
            dve.tensor_copy(b2_part[:, 1, :], b2_rest[:, 0, :]).then_inc(b_parts, 1)
            dve.wait_ge(b_parts, 3)
            dve.tensor_tensor(b2_rest[:, 1, :], b2_rest[:, 0, :], b2_part[:, 1, :], ALU.subtract).then_inc(b_parts, 1)
            dve.wait_ge(b_parts, 4)
            dve.tensor_copy(b2_part[:, 2, :], b2_rest[:, 1, :]).then_inc(b_parts, 1)
            for g in range(1, GROUPS):
                layer_norm(g)
                route(g)
                weights(g)
                attention(2 * g - 2)
                place_rows(g)
                if g == GROUPS - 1:
                    tile_counts()
                    tile_table(0)
                attention(2 * g - 1)
            tile_table(1)
            attention(STEPS - 2)
            attention(STEPS - 1)
            attention(STEPS)

            ps = passes[0]

            def step1(t, turn, j, _=None, fresh=False):
                a, b = row_in[j], row_out[j]
                if not fresh:
                    dve.wait_ge(ps.sent[j], 16 * turn)
                dve.wait_ge(ps.o_psum, t + 1)
                eo = ps_o[j % 2][:, 0:P]
                dve.scalar_tensor_tensor(b[:, 0:P], eo, 0.5, a[:, 0:P], ALU.mult, ALU.add)
                dve.scalar_tensor_tensor(b[:, P:2 * P], eo, a[:, P + 1:P + 2], a[:, 0:P], ALU.mult, ALU.add)\
                    .then_inc(ps.o_read, 1)
                dve.tensor_copy(b[:, 2 * P:2 * P + 2], a[:, P + 2:P + 4])
                dve.tensor_copy(place[j][:, :], a[:, P:P + 1]).then_inc(ps.row_done, 1)

            for t in range(RING):
                step1(t, 0, t, fresh=True)
            tiles(dve, RING, EXPERT_TILES, step1)

            ps2 = passes[1]

            def mix(t, turn, j, tail):
                a, c = row_in[j], j % 2
                dve.wait_ge(ps2.o_psum, t + 1)
                dve.scalar_tensor_tensor(res[c][:, :], ps_o[c][:, 0:P], a[:, 2 * P:2 * P + 1], a[:, P:2 * P],
                                         ALU.mult, ALU.add).then_inc(ps2.o_read, 1)
                if tail:
                    tail[0]()
                dve.wait_ge(ps2.o_read, t + 1)
                dve.bn_stats(st2[c][:, :], res[c][:, :]).then_inc(ps2.stats, 1)
                dve.wait_ge(ps2.stats, t + 1)
                if tail:
                    tail[1]()
                dve.bn_aggr(mv2[c][:, :], st2[c][:, :]).then_inc(ps2.moments, 1)
                if tail:
                    tail[2]()

            def tail_of(t, turn, j, fresh=False):
                a, b, c = row_in[j], row_out[j], j % 2

                def centre():
                    dve.wait_ge(ps2.moments, t + 1)
                    dve.scalar_tensor_tensor(cent[c][:, :], res[c][:, :], mv2[c][:, 0:1], gamma_bc[:, :],
                                             ALU.subtract, ALU.mult).then_inc(ps2.cent, 1)

                def invert():
                    dve.wait_ge(ps2.std, t + 1)
                    dve.reciprocal(rstd2[c][:, :], std2[c][:, :]).then_inc(ps2.rstd, 1)

                def finish():
                    if not fresh:
                        dve.wait_ge(ps2.sent[j], 16 * turn)
                    else:
                        dve.wait_ge(passes[0].sent[j], 16 * len(range(j, EXPERT_TILES, RING)))
                    dve.tensor_copy(place[j][:, :], a[:, 2 * P + 1:2 * P + 2])
                    dve.wait_ge(ps2.cent, t + 1)
                    dve.wait_ge(ps2.rstd, t + 1)
                    dve.scalar_tensor_tensor(b[:, 0:P], cent[c][:, :], rstd2[c][:, 0:1], beta_bc[:, :],
                                             ALU.mult, ALU.add).then_inc(ps2.row_done, 1)

                return centre, invert, finish

            mix(0, 0, 0, None)
            for t in range(1, RING + 1):
                mix(t, t // RING, t % RING, tail_of(t - 1, 0, t - 1, fresh=True))

            def step2(t, turn, j, _):
                mix(t, turn, j, tail_of(t - 1, turn - (j == 0), (j - 1) % RING))

            tiles(dve, RING + 1, EXPERT_TILES, step2)
            t = EXPERT_TILES - 1
            for part in tail_of(t, t // RING, t % RING):
                part()

            for n in range(STEPS):
                dve.wait_ge(silu_done, n + 1)
                dve.tensor_tensor(cols(z, n * ST, ST), cols(z, n * ST, ST), cols(s, n * ST, ST), ALU.mult)\
                    .then_inc(gated, 1)
                dve.wait_ge(gated, n + 1)
                dve.tensor_tensor(cols(z, n * ST, ST), cols(z, n * ST, ST), cols(x, n * ST, ST), ALU.add)\
                    .then_inc(out_done, 1)


def kernel(L0_attn_query, L0_attn_W_qkv, L0_attn_b_qkv, L0_attn_W_out, L0_attn_b_out, L0_attn_weight_q,
           L0_attn_weight_v, L0_ffn_gate_W, L0_ffn_gate_b, L0_ffn_W1, L0_ffn_b1, L0_ffn_W2, L0_ffn_b2,
           L0_ffn_ln_gamma, L0_ffn_ln_beta):
    import concourse.bacc as bacc
    from concourse.bass_utils import run_bass_kernel_spmd

    a = np.asarray
    wqkv, bqkv = a(L0_attn_W_qkv), a(L0_attn_b_qkv)
    arrays = {
        "query": a(L0_attn_query),
        "wq_t": wqkv[0:P].T, "wv_t": wqkv[2 * P:3 * P].T, "bq": bqkv[0:P], "bv": bqkv[2 * P:3 * P],
        "wo_t": a(L0_attn_W_out).T, "bo": a(L0_attn_b_out),
        "weight_q": a(L0_attn_weight_q).transpose(0, 2, 1).reshape(P, 3),
        "weight_v": a(L0_attn_weight_v).transpose(0, 2, 1).reshape(P, 3),
        "gate_w": a(L0_ffn_gate_W), "gate_b": a(L0_ffn_gate_b),
        "w1": a(L0_ffn_W1), "w2": a(L0_ffn_W2),
        "b1": a(L0_ffn_b1).reshape(E, 2, P).transpose(2, 0, 1), "b2": a(L0_ffn_b2),
        "gamma": a(L0_ffn_ln_gamma), "beta": a(L0_ffn_ln_beta),
    }
    arrays.update(consts())
    arrays = {n: np.ascontiguousarray(v) for n, v in arrays.items()}
    nc = bacc.Bacc("TRN2", target_bir_lowering=False, num_devices=1)
    io = {n: nc.dram_tensor(f"in_{n}", v.shape, mybir.dt.from_np(v.dtype), kind="ExternalInput").ap()
          for n, v in arrays.items()}
    out = nc.dram_tensor("out", (16, 256, P), F32, kind="ExternalOutput").ap()
    build(nc, io, out)
    r = run_bass_kernel_spmd(nc, [{f"in_{n}": v for n, v in arrays.items()}], core_ids=[0])
    return r.results[0]["out"]
```

```python
from contextlib import ExitStack

import numpy as np

import concourse.bass as bass
from concourse import mybir

F32 = mybir.dt.float32
BF16 = mybir.dt.bfloat16
I32 = mybir.dt.int32
U32 = mybir.dt.uint32
ALU = mybir.AluOpType
ACT = mybir.ActivationFunctionType
AX_X = mybir.AxisListType.X

P = 128
E = 8
H = 256
TOKENS = 16 * 256
TILES = TOKENS // P
GT = 8
GROUPS = TILES // GT
ST = 4
STEPS = TILES // ST
K = 2
REG = TOKENS + P
ROWS = (E + 1) * REG
EXPERT_TILES = TILES - 1 + E
RING = 8
NORM_V = (5, 2, 2, 2)
BEFORE = 4
BETWEEN = 5
WARM_START = 14
WARM_GATE = 4
POOL_GATES = (0, 2, 4)
GATE_N = 64
GATE_FROM = 6
LN_GROUPS = ((0, 1), (1, 2), (2, GROUPS))
TABLE = 48
W1_COLS = H + 2
ROW1 = P + 4
ROW2 = 2 * P + 2
NOWHERE = 1.0e6
EPS = 1e-5
C1 = 0.7071067811865476


def haar_matrix():
    c = np.float32(C1)
    m = np.zeros((P, P), np.float32)
    for k in range(P // 8):
        m[8 * k:8 * k + 8, k] = c * c * c
        m[8 * k:8 * k + 4, 16 + k] = c * c * c
        m[8 * k + 4:8 * k + 8, 16 + k] = -c * c * c
    for k in range(P // 4):
        m[4 * k:4 * k + 2, 32 + k] = c * c
        m[4 * k + 2:4 * k + 4, 32 + k] = -c * c
    for k in range(P // 2):
        m[2 * k, 64 + k] = c
        m[2 * k + 1, 64 + k] = -c
    return m


LEVELS = ((0, 16), (16, 32), (32, 64), (64, 128))


def consts():
    pad1 = np.zeros((P, ROW1), np.float32)
    pad1[:, P] = pad1[:, P + 3] = NOWHERE
    pad2 = np.zeros((P, ROW2), np.float32)
    pad2[:, 2 * P + 1] = NOWHERE
    p, t = np.arange(P), np.arange(TILES)
    line = np.concatenate([np.arange(E), np.tile(np.arange(E) * REG, K),
                           np.tril(np.ones((E, E))).ravel(), np.arange(EXPERT_TILES)]).astype(np.float32)
    square = {"identity": np.eye(P), "haar": haar_matrix(), "before": np.triu(np.ones((P, P)), 1),
              "tok": t[None, :] * P + p[:, None], "lines": np.tile(line, (P, 1))}
    return {"consts": np.concatenate([np.asarray(v, np.float32) for v in square.values()], axis=1),
            "haar_t": np.ascontiguousarray(haar_matrix().T), "pad1": pad1, "pad2": pad2}


def build(nc, io, out):
    ctx = ExitStack()
    with ctx:
        def sb(name, shape, dt=F32):
            return ctx.enter_context(nc.sbuf_tensor(name, shape, dt))

        def sem(name):
            return ctx.enter_context(nc.semaphore(name))

        rows1_dram = nc.dram_tensor("rows1", [ROWS, ROW1], F32).ap()
        rows2_dram = nc.dram_tensor("rows2", [ROWS, ROW2], F32).ap()
        z_dram = nc.dram_tensor("z_by_token", [TOKENS, P], F32).ap()
        b2_dram = nc.dram_tensor("b2_parts", [3, E, P], BF16).ap()

        wq, wv, wo = (sb(n, [P, P]) for n in ("wq", "wv", "wo"))
        vectors_bc = sb("vectors_bc", [P, 3 * P])
        bo_bc, gamma_bc, beta_bc = (vectors_bc[:, n * P:(n + 1) * P] for n in range(3))
        gw = sb("gw", [P, GATE_N])
        gb_bc = sb("gb_bc", [P, E])
        att_cols = sb("att_cols", [P, 8])
        att_scale = sb("att_scale", [P, 6])
        haar_t = sb("haar_t_sb", [P, P])
        before = sb("before_sb", [P, P], BF16)
        ones = sb("ones", [P, P], BF16)
        LINE = E + K * E + E * E + EXPERT_TILES
        consts_sb = sb("consts_sb", [P, 3 * P + TILES + LINE])
        ident, haar, before_f = (consts_sb[:, n * P:(n + 1) * P] for n in range(3))
        tok = consts_sb[:, 3 * P:3 * P + TILES]
        lines = consts_sb[:, 3 * P + TILES:]
        iota_e = lines[:, 0:E]
        region = lines[:, E:E + K * E]
        tril = lines[:, E + K * E:E + K * E + E * E]
        iota_t = lines[:, E + K * E + E * E:]
        pad1, pad2 = sb("pad1_sb", [P, ROW1]), sb("pad2_sb", [P, ROW2])
        eps_col = sb("eps_col", [P, 1])
        warm = sb("warm", [P, 1])
        w2 = sb("w2_sb", [P, E * 2 * P])
        w1_all = sb("w1_all", [P, E * W1_COLS])
        w1 = [sb(f"w1_{j}", [P, W1_COLS]) for j in range(4)]
        b2_row = sb("b2_row", [E, P])
        b2_rest = sb("b2_rest", [E, 2, P])
        b2_part = sb("b2_part", [E, 3, P], BF16)
        b2 = sb("b2_sb", [P, E * P], BF16)

        x = sb("x", [P, TILES * P])
        s = sb("s", [P, TILES * P])

        rows = [sb(f"rows_{b}", [P, GT, ROW1]) for b in range(GROUPS)]
        slot1 = [sb(f"slot1_{b}", [P, GT], I32) for b in range(GROUPS)]
        stats = sb("stats", [P, TILES, 6])
        moments = sb("moments", [P, TILES, 2])
        dev = sb("dev", [P, TILES])
        rstd = sb("rstd", [P, TILES])
        shift = sb("shift", [P, TILES])
        xt = [sb(f"xt_{u}", [P, ST * P]) for u in range(2)]
        hx = [sb(f"hx_{n}", [P, ST * P]) for n in range(STEPS)]
        logits = sb("logits", [P, GT, E])
        top = sb("top", [P, GT, 8])
        top_at = sb("top_at", [P, GT, 8], U32)
        onehot = sb("onehot", [P, GT, K, E], BF16)
        shifted = sb("shifted", [P, GT, E + 1])
        expd = sb("expd", [P, GT, E + 1])
        total = sb("total", [P, GT])
        places = sb("places", [P, GT, K * E])
        chosen = sb("chosen", [P, GT, K, E])
        slots = sb("slots", [P, GT, K])
        carry = sb("carry", [P, K * E])
        qw = [sb(f"qw_{b}", [P, ST * P]) for b in range(2)]
        prod = [sb(f"prod_{b}", [P, ST * P]) for b in range(2)]
        y_sb = [sb(f"y_sb_{b}", [P, ST * P]) for b in range(2)]

        counts = sb("counts", [1, K * E])
        counts_i = sb("counts_i", [1, K * E], I32)
        n_tiles = sb("n_tiles", [1, K * E])
        tri = sb("tri", [1, K, E, E])
        ends = sb("ends", [1, K, E])
        past = sb("past", [1, K, EXPERT_TILES, E])
        past_n = sb("past_n", [1, K, EXPERT_TILES, E])
        t_expert = sb("t_expert", [1, K, EXPERT_TILES])
        t_start = sb("t_start", [1, K, EXPERT_TILES])
        t_row = sb("t_row", [1, K, EXPERT_TILES])
        table_row = sb("table_row", [1, K * TABLE], I32)
        table_expert = sb("table_expert", [1, K * TABLE], I32)
        pad_at = sb("pad_at", [1, K * E], I32)

        row_in = [sb(f"row_in_{j}", [P, ROW2]) for j in range(RING)]
        row_out = [sb(f"row_out_{j}", [P, ROW2]) for j in range(RING)]
        place = [sb(f"place_{j}", [P, 1], I32) for j in range(RING)]
        et = [sb(f"et_{b}", [P, P]) for b in range(2)]
        hid = [sb(f"hid_{b}", [P, 2 * P]) for b in range(2)]
        res = [sb(f"res_{b}", [P, P]) for b in range(2)]
        cent = [sb(f"cent_{b}", [P, P]) for b in range(4)]
        st2 = [sb(f"st2_{b}", [P, 6]) for b in range(2)]
        mv2 = [sb(f"mv2_{b}", [P, 2]) for b in range(2)]
        std2 = [sb(f"std2_{b}", [P, 1]) for b in range(2)]
        rstd2 = [sb(f"rstd2_{b}", [P, 1]) for b in range(2)]
        z = sb("z", [P, TILES * P])

        bank = [ctx.enter_context(nc.psum_tensor(f"bank{i}", [P, 512], F32)) for i in range(8)]
        ps_x, ps_lg, ps_rk, ps_q, ps_v, ps_y, ps_s = bank[0:2], bank[2], bank[3], bank[4], bank[5], bank[6], bank[7]
        ps_t, ps_h, ps_o = bank[0:2], bank[2:4], bank[4:6]

        x_in = [sem(f"x_in_{g}") for g in range(GROUPS + 1)]
        const_in = sem("const_in")
        att_in = sem("att_in")
        late_in = sem("late_in")
        b_in = sem("b_in")
        zeroed = sem("zeroed")
        set_up = sem("set_up")
        b_parts = sem("b_parts")
        b_stored = sem("b_stored")
        b_loaded = sem("b_loaded")
        stats_done = sem("stats_done")
        moments_done = sem("moments_done")
        dev_done = sem("dev_done")
        rstd_done = sem("rstd_done")
        shift_done = sem("shift_done")
        xn_done = sem("xn_done")
        xn_act = sem("xn_act")
        gate_in = sem("gate_in")
        gate_bias_in = sem("gate_bias_in")
        xt_psum = sem("xt_psum")
        xt_sbuf = sem("xt_sbuf")
        logits_psum = sem("logits_psum")
        logits_sbuf = sem("logits_sbuf")
        top_done = sem("top_done")
        top_at_done = sem("top_at_done")
        onehot_done = sem("onehot_done")
        shifted_done = sem("shifted_done")
        exp_done = sem("exp_done")
        total_done = sem("total_done")
        weight1_done = sem("weight1_done")
        rank_psum = sem("rank_psum")
        places_done = sem("places_done")
        carry_done = sem("carry_done")
        chosen_done = sem("chosen_done")
        slots_done = sem("slots_done")
        meta_done = sem("meta_done")
        sent = [sem(f"sent_{b}") for b in range(GROUPS)]
        hx_psum = sem("hx_psum")
        hx_sbuf = sem("hx_sbuf")
        q_psum = sem("q_psum")
        v_psum = sem("v_psum")
        qw_done = sem("qw_done")
        prod_done = sem("prod_done")
        y_psum = sem("y_psum")
        y_sbuf = sem("y_sbuf")
        s_psum = sem("s_psum")
        s_sbuf = sem("s_sbuf")
        table_step = sem("table_step")
        table_done = sem("table_done")
        pads_known = sem("pads_known")
        pads1 = sem("pads1")
        pads2 = sem("pads2")

        class Pass:
            def __init__(self, k):
                self.k = k
                self.rows_in = [sem(f"p{k}_rows_in_{j}") for j in range(RING)]
                self.sent = [sem(f"p{k}_sent_{j}") for j in range(RING)]
                self.et_psum = sem(f"p{k}_et_psum")
                self.et_sbuf = sem(f"p{k}_et_sbuf")
                self.hid_psum = sem(f"p{k}_hid_psum")
                self.hid_sbuf = sem(f"p{k}_hid_sbuf")
                self.o_psum = sem(f"p{k}_o_psum")
                self.o_read = sem(f"p{k}_o_read")
                self.row_done = sem(f"p{k}_row_done")
                self.row_read = self.row_done if k == 0 else sem(f"p{k}_row_read")
                self.scattering = sem(f"p{k}_scattering")
                if k == 1:
                    self.stats = sem(f"p{k}_stats")
                    self.moments = sem(f"p{k}_moments")
                    self.std = sem(f"p{k}_std")
                    self.rstd = sem(f"p{k}_rstd")
                    self.cent = sem(f"p{k}_cent")

        passes = [Pass(0), Pass(1)]
        def tail_order():
            gated_steps = 0
            for n in range(BETWEEN, STEPS + 1):
                yield "attention", n
                while n >= GATE_FROM and gated_steps < min(2 * (n - GATE_FROM + 1), n):
                    yield "gate", gated_steps
                    gated_steps += 1
            for n in range(gated_steps, STEPS):
                yield "gate", n

        z_in = [sem(f"z_in_{n}") for n in range(STEPS)]
        silu_done = sem("silu_done")
        gated = [sem(f"gated_{n}") for n in range(STEPS)]
        out_stored = sem("out_stored")

        query_v = io["query"].rearrange("b l d -> (b l) d").rearrange("(t p) d -> p t d", p=P)
        out_v = out.rearrange("b l d -> (b l) d").rearrange("(t p) d -> p t d", p=P)
        z_v = z_dram.rearrange("(t p) d -> p t d", p=P)

        def cols(ap, t, n=1):
            return ap[:, t * P:(t + n) * P]

        def by_tile(ap, n):
            return ap.rearrange("p (t c) -> p t c", t=n)

        def entries(eng, table, k, first, n):
            top = (E - 1) if table is table_expert else E * REG
            width = E if table is pad_at else TABLE
            _, values = nc.values_load_multi_w_load_instructions(
                table[0:1, bass.ds(first + k * width, n)], engines=[eng.engine], min_val=0, max_val=top,
                skip_runtime_bounds_check_because="VectorE clamps every entry to this range")
            return values

        def fill(eng, k, dst, pad, done):
            for at in entries(eng, pad_at, k, 0, E):
                eng.dma_start(dst[bass.ds(at, P), :], pad[:, :]).then_inc(done, 16)

        def tiles(eng, first, end, step, table=None, k=0, ahead=0):
            def turn(t0, i, n):
                loaded = []

                def entry(j):
                    if not loaded:
                        loaded.extend(entries(eng, table, k, t0 + ahead, n))
                    return loaded[j]

                for j in range(n):
                    step(t0 + j, i + (first + j) // RING, (first + j) % RING, lambda j=j: entry(j))

            loops = (end - first) // RING
            with eng.Fori(0, loops) as i:
                turn(i * RING + first, i, RING)
            rest = first + loops * RING
            if rest < end:
                turn(rest, loops, end - rest)

        def haar_beside(n):
            return {0: (GROUPS, GROUPS + 1), 1: (GROUPS + 2,), 2: (GROUPS + 3,)}.get(n, ())

        def gate_step(eng, n):
            eng.wait_ge(silu_done, n + 1)
            eng.wait_ge(s_sbuf, n + 1)
            eng.tensor_tensor(cols(z, n * ST, ST), cols(z, n * ST, ST), cols(s, n * ST, ST), ALU.mult)\
                .then_inc(gated[n], 1)
            eng.wait_ge(gated[n], 1)
            eng.tensor_tensor(cols(z, n * ST, ST), cols(z, n * ST, ST), cols(x, n * ST, ST), ALU.add)\
                .then_inc(gated[n], 1)

        block = ctx.enter_context(nc.Block())

        @block.sync
        def _(sp):
            sp.dma_start(by_tile(cols(x, 0, ST), ST), query_v[:, 0:ST, :]).then_inc(x_in[0], 16)
            for g in range(1, GROUPS):
                sp.dma_start(by_tile(cols(x, g * GT, GT), GT), query_v[:, g * GT:(g + 1) * GT, :])\
                    .then_inc(x_in[g + 1], 16)
            loads = [(wq[:, :], io["wq_t"]), (wv[:, :], io["wv_t"]), (wo[:, :], io["wo_t"]),
                     (haar_t[:, :], io["haar_t"]), (att_cols[:, :], io["att_cols"]),
                     (vectors_bc[:, :], io["vectors"].rearrange("(a n) -> a n", a=1).to_broadcast([P, 3 * P]))]
            for dst, src in loads:
                sp.dma_start(dst, src).then_inc(att_in, 16)
            sp.dma_start(b2_row[:, :], io["b2"]).then_inc(b_in, 16)
            late = [(w2[:, :].rearrange("p (e c d) -> p e c d", e=E, c=2),
                     io["w2"].rearrange("e (c p) d -> p e c d", p=P)),
                    (w1_all[:, :].rearrange("p (e h) -> p e h", e=E)[:, :, 0:H], io["w1"].rearrange("e p h -> p e h")),
                    (w1_all[:, :].rearrange("p (e h) -> p e h", e=E)[:, :, H:W1_COLS], io["b1"]),
                    (pad1[:, :], io["pad1"]), (pad2[:, :], io["pad2"])]
            for dst, src in late:
                sp.dma_start(dst, src).then_inc(late_in, 16)
            sp.wait_ge(late_in, 16 * 5)
            sp.dma_start(rows1_dram[E * REG:E * REG + P, :], pad1[:, :]).then_inc(pads1, 16)
            sp.dma_start(rows2_dram[E * REG:E * REG + P, :], pad2[:, :]).then_inc(pads2, 16)
            sp.wait_ge(b_parts, 5)
            for k in range(3):
                sp.dma_start(b2_dram[k], b2_part[:, k, :]).then_inc(b_stored, 16)
            sp.wait_ge(b_stored, 48)
            sp.wait_ge(zeroed, 1)
            sp.dma_start(b2[0:3, :], b2_dram.rearrange("k e n -> k (e n)")).then_inc(b_loaded, 16)
            sp.wait_ge(pads_known, 1)
            fill(sp, 0, rows1_dram, pad1, pads1)
            fill(sp, 1, rows2_dram, pad2, pads2)

            for ps in passes:
                src, width = (rows1_dram, ROW1) if ps.k == 0 else (rows2_dram, ROW2)

                def load_rows(t, turn, j, row):
                    sp.dma_start(row_in[j][:, 0:width], src[bass.ds(row, P), :]).then_inc(ps.rows_in[j], 16)

                sp.wait_ge(table_done, ps.k + 1)
                first = entries(sp, table_row, ps.k, 0, RING)
                if ps.k == 0:
                    for g in range(GROUPS):
                        sp.wait_ge(sent[g], 16 * GT)
                    sp.wait_ge(pads1, 16 * (E + 1))
                else:
                    for j in range(RING):
                        sp.wait_ge(passes[0].sent[j], 16 * len(range(j, EXPERT_TILES, RING)))
                    sp.wait_ge(pads2, 16 * (E + 1))
                    sp.wait_ge(passes[0].row_read, EXPERT_TILES)
                for t, row in enumerate(first):
                    load_rows(t, 0, t, row)

                def step(t, turn, j, row):
                    row = row()
                    sp.wait_ge(ps.row_read, t - RING + 1)
                    load_rows(t, turn, j, row)

                tiles(sp, RING, EXPERT_TILES, step, table_row, ps.k)

            for j in range(RING):
                sp.wait_ge(passes[1].sent[j], 16 * len(range(j, EXPERT_TILES, RING)))
            for n in range(STEPS):
                sp.dma_start(by_tile(cols(z, n * ST, ST), ST), z_v[:, n * ST:(n + 1) * ST, :]).then_inc(z_in[n], 16)
            for n in range(STEPS):
                sp.wait_ge(gated[n], 2)
                sp.dma_start(out_v[:, n * ST:(n + 1) * ST, :], by_tile(cols(z, n * ST, ST), ST))\
                    .then_inc(out_stored, 16)
            sp.wait_ge(out_stored, 16 * STEPS)

        @block.gpsimd
        def _(pool):
            pool.memset(b2[:, :].bitcast(I32), 0).then_inc(zeroed, 1)
            pool.memset(ones[:, :], 1.0).then_inc(zeroed, 1)
            pool.memset(gw[:, :], 0.0).then_inc(zeroed, 1)
            pool.memset(eps_col[:, :], EPS).then_inc(zeroed, 1)
            for g in range(GROUPS):
                pool.wait_ge(meta_done, g + 1)
                for t in range(GT):
                    pool.indirect_dma_start(
                        out=rows1_dram[:, :], out_offset=bass.IndirectOffsetOnAxis(ap=slot1[g][:, t:t + 1], axis=0),
                        in_=rows[g][:, t, :], in_offset=None,
                        bounds_check=ROWS - 1, oob_is_err=False).then_inc(sent[g], 16)
            for ps in passes:
                dst, width, last = (rows2_dram, ROW2, ROWS - 1) if ps.k == 0 else (z_dram, P, TOKENS - 1)

                def step(t, turn, j, _):
                    pool.wait_ge(ps.row_done, t + 1)
                    pool.sem_inc(ps.scattering, 1)
                    pool.indirect_dma_start(
                        out=dst[:, :], out_offset=bass.IndirectOffsetOnAxis(ap=place[j][:, 0:1], axis=0),
                        in_=row_out[j][:, 0:width], in_offset=None,
                        bounds_check=last, oob_is_err=False).then_inc(ps.sent[j], 16)

                tiles(pool, 0, EXPERT_TILES, step)
            for n in POOL_GATES:
                gate_step(pool, n)

        @block.tensor
        def _(pe):
            def transposes(g):
                for u in range(2):
                    if g > u + 1:
                        pe.wait_ge(hx_sbuf, g - 1 - (g - u) % 2)
                    for t in range(ST):
                        at = ST * u + t
                        if at < NORM_V[g]:
                            pe.wait_ge(xn_done, sum(NORM_V[:g]) + at + 1)
                        else:
                            pe.wait_ge(xn_act, GT * g + at + 1 - sum(NORM_V[:g + 1]))
                        mm = pe.transpose(cols(ps_x[u], t), rows[g][:, ST * u + t, 0:P], ident[:, :])
                    mm.then_inc(xt_psum, 1)

            def gate(g):
                if g:
                    pe.wait_ge(logits_sbuf, g)
                for u in range(2):
                    pe.wait_ge(xt_sbuf, 2 * g + u + 1)
                    for t in range(ST):
                        at = (ST * u + t) * GATE_N
                        mm = pe.matmul(ps_lg[:, at:at + GATE_N], cols(xt[u], t), gw[:, :], start=True, stop=True)
                mm.then_inc(logits_psum, 1)

            def haar_coefs(n):
                if n < GROUPS:
                    pe.wait_ge(xt_sbuf, 2 * min(n + 1, GROUPS - 1) + n % 2 + 1)
                if n >= 2:
                    pe.wait_ge(hx_sbuf, n - 1)
                for t in range(ST):
                    at = ST * n + t
                    mm = pe.matmul(cols(ps_x[n % 2], t), rows[at // GT][:, at % GT, 0:P], haar[:, :],
                                   start=True, stop=True)
                mm.then_inc(hx_psum, 1)

            def ranks(g):
                pe.wait_ge(onehot_done, g + 1)
                if g:
                    pe.wait_ge(carry_done, g)
                    pe.wait_ge(places_done, g)
                oh = onehot[:, :, :, :].rearrange("p t k e -> p t (k e)")
                n = K * E
                for t in range(GT):
                    pe.matmul(ps_rk[:, GT * n:GT * n + n], ones[:, :], oh[:, t, :], start=(t == 0), stop=(t == GT - 1))
                mm = pe.matmul(ps_rk[:, 0:GT * n], before[:, :], oh.rearrange("p t n -> p (t n)"),
                               start=True, stop=False, skip_group_check=True)
                for t in range(GT - 1):
                    later = GT - 1 - t
                    mm = pe.matmul(ps_rk[:, (t + 1) * n:GT * n].rearrange("p (t n) -> p t n", t=later), ones[:, :],
                                   oh[:, t:t + 1, :].to_broadcast([P, later, n]), start=False,
                                   stop=(t == GT - 2), skip_group_check=True)
                mm.then_inc(rank_psum, 1)

            def q_of(n):
                if n:
                    pe.wait_ge(qw_done, n)
                pe.wait_ge(hx_sbuf, n + 1)
                pe.matmul(ps_q[:, :], wq[:, :], hx[n][:, :], start=True, stop=True).then_inc(q_psum, 1)

            def v_of(n):
                if n:
                    pe.wait_ge(prod_done, n)
                pe.matmul(ps_v[:, :], wv[:, :], hx[n][:, :], start=True, stop=True).then_inc(v_psum, 1)

            def y_of(n):
                pe.wait_ge(prod_done, n + 1)
                if n:
                    pe.wait_ge(y_sbuf, n)
                for t in range(ST):
                    mm = pe.matmul(cols(ps_y, t), cols(prod[n % 2], t), wo[:, :], start=True, stop=True)
                mm.then_inc(y_psum, 1)

            def s_of(n):
                pe.wait_ge(y_sbuf, n + 1)
                if n:
                    pe.wait_ge(s_sbuf, n)
                pe.matmul(ps_s[:, :], haar_t[:, :], y_sb[n % 2][:, :], start=True, stop=True).then_inc(s_psum, 1)

            def attention(n):
                if 0 < n < STEPS:
                    q_of(n)
                if n:
                    y_of(n - 1)
                if n < STEPS:
                    v_of(n)
                if n:
                    s_of(n - 1)
                for later in haar_beside(n):
                    haar_coefs(later)

            def keep_warm(n):
                for _ in range(n):
                    pe.matmul(ps_s[:, :], ones[:, :], ones[:, None, :].to_broadcast([P, 4, P]), start=True, stop=True)

            pe.wait_ge(zeroed, 4)
            keep_warm(WARM_START)
            pe.wait_ge(const_in, 16)
            pe.wait_ge(gate_in, 16)
            for g in range(GROUPS):
                transposes(g)
                if g == 1:
                    keep_warm(WARM_GATE)
                gate(g)
                if g:
                    haar_coefs(g - 1)
                if g == 0:
                    pe.wait_ge(set_up, 1)
                if g == GROUPS - 1:
                    pe.wait_ge(att_in, 16 * 6)
                    q_of(0)
                ranks(g)
            haar_coefs(GROUPS - 1)
            for n in range(BEFORE):
                attention(n)

            pe.wait_ge(b_loaded, 16)
            pe.wait_ge(late_in, 16 * 5)
            pe.wait_ge(hx_sbuf, STEPS)
            for ps in passes:
                def turn_rows(turn, j):
                    pe.wait_ge(ps.rows_in[j], 16 * (turn + 1))
                    pe.transpose(ps_t[j % 2][:, 0:P], row_in[j][:, 0:P], ident[:, :]).then_inc(ps.et_psum, 1)

                def layer1(t, j):
                    pe.wait_ge(ps.et_sbuf, t + 1)
                    for c in range(2):
                        mm = pe.matmul(cols(ps_h[j % 2], c), cols(w1[j % 4], c), et[j % 2][:, :], start=True, stop=True)
                    mm.then_inc(ps.hid_psum, 1)

                def layer2(t, j, expert, fresh=False):
                    pe.wait_ge(ps.hid_sbuf, t + 1)
                    if not fresh:
                        pe.wait_ge(ps.o_read, t - 1)
                    o = ps_o[j % 2][:, 0:P]
                    for c in range(2):
                        pe.matmul(o, cols(hid[j % 2], c), w2[:, bass.ds(expert * 2 * P + c * P, P)],
                                  start=(c == 0), stop=False)
                    pe.matmul(o, ones[:, :], b2[:, bass.ds(expert * P, P)],
                              start=False, stop=True).then_inc(ps.o_psum, 1)

                if ps.k == 1:
                    pe.wait_ge(passes[0].o_read, EXPERT_TILES)
                    for n in range(BEFORE, BETWEEN):
                        attention(n)
                pe.wait_ge(table_done, ps.k + 1)
                first = entries(pe, table_expert, ps.k, 0, 4)
                turn_rows(0, 0)
                turn_rows(0, 1)
                layer1(0, 0)
                turn_rows(0, 2)
                pe.wait_ge(prod_done, BEFORE if ps.k == 0 else BETWEEN)
                for t in range(1, 3):
                    layer1(t, t)
                    turn_rows(0, t + 2)
                    layer2(t - 1, t - 1, first[t - 1], fresh=True)

                def step(t, turn, j, expert, ahead=True):
                    layer1(t, j)
                    if ahead:
                        turn_rows(turn + (j + 2) // RING, (j + 2) % RING)
                    layer2(t - 1, (j - 1) % RING, expert())

                last = EXPERT_TILES - 2 - (EXPERT_TILES - 2 - 3) % RING
                tiles(pe, 3, last, step, table_expert, ps.k, ahead=-1)
                left = entries(pe, table_expert, ps.k, last - 1, EXPERT_TILES - last + 1)
                for n, t in enumerate(range(last, EXPERT_TILES)):
                    step(t, t // RING, t % RING, lambda n=n: left[n], ahead=t + 2 < EXPERT_TILES)
                t = EXPERT_TILES - 1
                layer2(t, t % RING, left[-1])

            pe.wait_ge(passes[1].o_read, EXPERT_TILES)
            for n in range(BETWEEN, STEPS + 1):
                attention(n)

        @block.scalar
        def _(act):
            act.dma_start(by_tile(cols(x, ST, ST), ST), query_v[:, ST:2 * ST, :]).then_inc(x_in[1], 16)
            act.dma_start(consts_sb[:, :], io["consts"]).then_inc(const_in, 16)
            act.wait_ge(zeroed, 4)
            act.dma_start(gw[:, 0:E], io["gate_w"]).then_inc(gate_in, 16)
            act.dma_start(gb_bc[:, :], io["gate_b"].rearrange("(a n) -> a n", a=1).to_broadcast([P, E]))\
                .then_inc(gate_bias_in, 16)
            act.activation(warm[:, :], eps_col[:, 0:1], ACT.Sqrt)

            def deviations(n):
                act.wait_ge(moments_done, LN_GROUPS[n][1])
                t = slice(GT * LN_GROUPS[n][0], GT * LN_GROUPS[n][1])
                act.activation(dev[:, t], moments[:, t, 1], ACT.Sqrt, bias=eps_col[:, 0:1]).then_inc(dev_done, 1)

            def normalize(g):
                act.wait_ge(shift_done, sum(first <= g for first, _ in LN_GROUPS))
                for t in range(NORM_V[g], GT):
                    at = GT * g + t
                    act.activation(rows[g][:, t, 0:P], cols(x, at), ACT.Identity,
                                   bias=shift[:, at:at + 1], scale=rstd[:, at:at + 1]).then_inc(xn_act, 1)

            def xt_copy(g):
                for u in range(2):
                    act.wait_ge(xt_psum, 2 * g + u + 1)
                    if g:
                        act.wait_ge(logits_psum, g)
                    act.activation(xt[u][:, :], ps_x[u][:, :], ACT.Copy).then_inc(xt_sbuf, 1)

            def hx_copy(n):
                act.wait_ge(hx_psum, n + 1)
                act.activation(hx[n][:, :], ps_x[n % 2][:, :], ACT.Copy).then_inc(hx_sbuf, 1)

            def exps(g):
                act.wait_ge(shifted_done, g + 1)
                if g:
                    act.wait_ge(weight1_done, 2 * g)
                act.activation(expd[:, :, :], shifted[:, :, :], ACT.Exp).then_inc(exp_done, 1)

            def qw_of(n):
                act.wait_ge(q_psum, n + 1)
                if n >= 2:
                    act.wait_ge(prod_done, n - 1)
                src, dst = by_tile(ps_q[:, :], ST), by_tile(qw[n % 2][:, :], ST)
                for k, (a, b) in enumerate(LEVELS):
                    if k == 0:
                        ins = act.activation(dst[:, :, a:b], src[:, :, a:b], ACT.Identity,
                                             bias=att_scale[:, 0:1], scale=att_scale[:, 2:3])
                    elif k < 3:
                        ins = act.activation(dst[:, :, a:b], src[:, :, a:b], ACT.Copy, scale=att_scale[:, 2 + k:3 + k])
                    else:
                        ins = act.activation(dst[:, :, a:b], src[:, :, a:b], ACT.Copy)
                ins.then_inc(qw_done, 1)

            def y_copy(n):
                act.wait_ge(y_psum, n + 1)
                if n >= 2:
                    act.wait_ge(s_psum, n - 1)
                act.activation(y_sb[n % 2][:, :], ps_y[:, :], ACT.Copy).then_inc(y_sbuf, 1)

            def attention(n):
                if n < STEPS:
                    qw_of(n)
                if n:
                    y_copy(n - 1)
                for later in haar_beside(n):
                    hx_copy(later)

            deviations(0)
            normalize(0)
            xt_copy(0)
            deviations(1)
            act.activation(warm[:, :], eps_col[:, 0:1], ACT.Exp)
            normalize(1)
            exps(0)
            xt_copy(1)
            deviations(2)
            act.activation(warm[:, :], eps_col[:, 0:1], ACT.Exp)
            hx_copy(0)
            exps(1)
            normalize(2)
            for g in range(2, GROUPS):
                xt_copy(g)
                if g + 1 < GROUPS:
                    normalize(g + 1)
                hx_copy(g - 1)
                if g + 1 < GROUPS:
                    exps(g)
            exps(GROUPS - 1)
            hx_copy(GROUPS - 1)
            act.wait_ge(set_up, 4)
            for n in range(BEFORE):
                attention(n)
            act.wait_ge(late_in, 16 * 5)
            act.wait_ge(table_done, 1)

            for ps in passes:
                def turned(t, j, expert):
                    act.activation(w1[j % 4][:, :], w1_all[:, bass.ds(expert * W1_COLS, W1_COLS)], ACT.Copy)
                    act.wait_ge(ps.et_psum, t + 1)
                    act.activation(et[j % 2][:, :], ps_t[j % 2][:, 0:P], ACT.Copy).then_inc(ps.et_sbuf, 1)

                def relu(t, j, fresh=False):
                    act.wait_ge(ps.hid_psum, t + 1)
                    if not fresh:
                        act.wait_ge(ps.o_psum, t - 1)
                    for c in range(2):
                        ins = act.activation(cols(hid[j % 2], c), cols(ps_h[j % 2], c), ACT.Relu,
                                             bias=w1[j % 4][:, H + c:H + c + 1])
                    ins.then_inc(ps.hid_sbuf, 1)

                def deviation(t, j, fresh=False):
                    act.wait_ge(ps.moments, t + 1)
                    if not fresh:
                        act.wait_ge(ps.rstd, t - 1)
                    act.activation(std2[j % 2][:, :], mv2[j % 2][:, 1:2], ACT.Sqrt, bias=eps_col[:, 0:1])\
                        .then_inc(ps.std, 1)

                if ps.k == 1:
                    act.activation(warm[:, :], eps_col[:, 0:1], ACT.Sqrt)
                    for n in range(BEFORE, BETWEEN):
                        attention(n)
                    act.wait_ge(table_done, 2)
                first = entries(act, table_expert, ps.k, 0, 6)
                turned(0, 0, first[0])
                turned(1, 1, first[1])
                for t in range(4):
                    relu(t, t, fresh=t < 2)
                    turned(t + 2, t + 2, first[t + 2])
                    if ps.k == 1 and t >= 2:
                        deviation(t - 2, t - 2, fresh=True)

                def step(t, turn, j, expert):
                    relu(t, j)
                    if expert is not None:
                        turned(t + 2, (j + 2) % RING, expert())
                    if ps.k == 1:
                        deviation(t - 2, (j - 2) % RING)

                tiles(act, 4, EXPERT_TILES - 2, step, table_expert, ps.k, ahead=2)
                for t in range(EXPERT_TILES - 2, EXPERT_TILES):
                    step(t, t // RING, t % RING, None)
                if ps.k == 1:
                    for t in range(EXPERT_TILES - 2, EXPERT_TILES):
                        deviation(t, t % RING)

            for what, n in tail_order():
                if what == "attention":
                    attention(n)
                    if n == BETWEEN:
                        act.activation(warm[:, :], eps_col[:, 0:1], ACT.Silu)
                else:
                    act.wait_ge(z_in[n], 16)
                    act.activation(cols(z, n * ST, ST), cols(z, n * ST, ST), ACT.Silu).then_inc(silu_done, 1)

        @block.vector
        def _(dve):
            def moments_of(g):
                dve.wait_ge(x_in[g + 1 if g else 0], 16)
                for t in range(GT * g, GT * g + GT):
                    if t == ST:
                        dve.wait_ge(x_in[1], 16)
                    ins = dve.bn_stats(stats[:, t, :], cols(x, t))
                ins.then_inc(stats_done, 1)
                dve.wait_ge(stats_done, g + 1)
                for t in range(GT * g, GT * g + GT):
                    ins = dve.bn_aggr(moments[:, t, :], stats[:, t, :])
                ins.then_inc(moments_done, 1)

            def rstd_of(n):
                t = slice(GT * LN_GROUPS[n][0], GT * LN_GROUPS[n][1])
                dve.wait_ge(dev_done, n + 1)
                dve.reciprocal(rstd[:, t], dev[:, t]).then_inc(rstd_done, 1)
                dve.wait_ge(rstd_done, n + 1)
                dve.scalar_tensor_tensor(shift[:, t], moments[:, t, 0], -1.0, rstd[:, t], ALU.mult, ALU.mult)\
                    .then_inc(shift_done, 1)

            def normalize(g):
                for t in range(NORM_V[g]):
                    at = GT * g + t
                    dve.tensor_scalar(rows[g][:, t, 0:P], cols(x, at), moments[:, at, 0:1],
                                      rstd[:, at:at + 1], ALU.subtract, ALU.mult).then_inc(xn_done, 1)

            def route(g):
                dve.wait_ge(logits_psum, g + 1)
                dve.tensor_tensor(logits[:, :, :], ps_lg[:, :].rearrange("p (t e) -> p t e", t=GT)[:, :, 0:E],
                                  gb_bc[:, None, :].to_broadcast([P, GT, E]), ALU.add).then_inc(logits_sbuf, 1)
                dve.wait_ge(logits_sbuf, g + 1)
                for t in range(GT):
                    ins = dve.max(top[:, t, :], logits[:, t, :])
                ins.then_inc(top_done, 1)
                dve.wait_ge(top_done, g + 1)
                for t in range(GT):
                    ins = dve.max_index(top_at[:, t, :], top[:, t, :], logits[:, t, :])
                ins.then_inc(top_at_done, 1)
                dve.tensor_tensor(shifted[:, :, 0:E], logits[:, :, :], top[:, :, 0:1].to_broadcast([P, GT, E]),
                                  ALU.subtract)
                dve.tensor_tensor(shifted[:, :, E], top[:, :, 1], top[:, :, 0], ALU.subtract)\
                    .then_inc(shifted_done, 1)
                dve.wait_ge(top_at_done, g + 1)
                if g:
                    dve.wait_ge(rank_psum, g)
                dve.tensor_tensor(onehot[:, :, :, :],
                                  iota_e[:, None, None, :].to_broadcast([P, GT, K, E]),
                                  top_at[:, :, 0:K][:, :, :, None].to_broadcast([P, GT, K, E]), ALU.is_equal)\
                    .then_inc(onehot_done, 1)

            def weights(g):
                dve.wait_ge(exp_done, g + 1)
                dve.tensor_reduce(total[:, :], expd[:, :, 0:E], AX_X, ALU.add).then_inc(total_done, 1)
                dve.wait_ge(total_done, g + 1)
                dve.reciprocal(rows[g][:, :, P + 1], total[:, :]).then_inc(weight1_done, 1)
                dve.wait_ge(weight1_done, 2 * g + 1)
                dve.tensor_tensor(rows[g][:, :, P + 2], expd[:, :, E], rows[g][:, :, P + 1], ALU.mult)\
                    .then_inc(weight1_done, 1)

            def place_rows(g):
                dve.wait_ge(rank_psum, g + 1)
                n = K * E
                dve.tensor_tensor(places[:, :, :], ps_rk[:, 0:GT * n].rearrange("p (t n) -> p t n", t=GT),
                                  carry[:, None, :].to_broadcast([P, GT, n]), ALU.add).then_inc(places_done, 1)
                dve.wait_ge(places_done, g + 1)
                dve.tensor_tensor(carry[:, :], carry[:, :], ps_rk[:, GT * n:GT * n + n], ALU.add)\
                    .then_inc(carry_done, 1)
                dve.tensor_tensor(chosen[:, :, :, :], places[:, :, :].rearrange("p t (k e) -> p t k e", k=K),
                                  onehot[:, :, :, :], ALU.mult).then_inc(chosen_done, 1)
                dve.wait_ge(chosen_done, g + 1)
                dve.tensor_reduce(slots[:, :, :], chosen[:, :, :, :], AX_X, ALU.add).then_inc(slots_done, 1)
                dve.tensor_copy(rows[g][:, :, P + 3], tok[:, g * GT:(g + 1) * GT])
                dve.wait_ge(slots_done, g + 1)
                dve.tensor_copy(rows[g][:, :, P], slots[:, :, 1])
                dve.tensor_copy(slot1[g][:, :], slots[:, :, 0]).then_inc(meta_done, 1)

            def attention(n):
                if n < STEPS:
                    dve.wait_ge(v_psum, n + 1)
                    dve.wait_ge(qw_done, n + 1)
                    if n >= 2:
                        dve.wait_ge(y_psum, n - 1)
                    v, q, o = (by_tile(a[:, :], ST) for a in (ps_v, qw[n % 2], prod[n % 2]))
                    b = LEVELS[0][1]
                    dve.scalar_tensor_tensor(o[:, :, 0:b], v[:, :, 0:b], att_scale[:, 1:2], q[:, :, 0:b],
                                             ALU.add, ALU.mult)
                    dve.tensor_tensor(o[:, :, b:P], v[:, :, b:P], q[:, :, b:P], ALU.mult).then_inc(prod_done, 1)
                if n:
                    dve.wait_ge(s_psum, n)
                    dve.tensor_tensor(by_tile(cols(s, (n - 1) * ST, ST), ST), by_tile(ps_s[:, :], ST),
                                      bo_bc[:, None, :].to_broadcast([P, ST, P]), ALU.add).then_inc(s_sbuf, 1)

            table_steps = [0]

            def table_next(ins):
                table_steps[0] += 1
                ins.then_inc(table_step, 1)
                dve.wait_ge(table_step, table_steps[0])

            def pad_places():
                dve.wait_ge(carry_done, GROUPS)
                dve.tensor_copy(pad_at[0:1, :], carry[0:1, :]).then_inc(pads_known, 1)

            def tile_counts():
                table_next(dve.tensor_tensor(counts[:, :], carry[0:1, :], region[0:1, :], ALU.subtract))
                table_next(dve.tensor_scalar(counts_i[:, :], counts[:, :], float(P - 1), None, ALU.add))
                table_next(dve.tensor_scalar(counts_i[:, :], counts_i[:, :], 7, None, ALU.logical_shift_right))
                table_next(dve.tensor_copy(n_tiles[:, :], counts_i[:, :]))
                for k in range(K):
                    nt = n_tiles[:, k * E:(k + 1) * E]
                    table_next(dve.tensor_tensor(tri[:, k, :, :], tril[0:1, :].rearrange("a (i j) -> a i j", i=E),
                                                 nt[:, None, :].to_broadcast([1, E, E]), ALU.mult))
                    table_next(dve.tensor_reduce(ends[:, k, :], tri[:, k, :, :], AX_X, ALU.add))

            def tile_table(k):
                shape = [1, EXPERT_TILES, E]
                nt = n_tiles[:, k * E:(k + 1) * E]
                it = iota_t[0:1, :]
                table_next(dve.tensor_tensor(past[:, k], it[:, :, None].to_broadcast(shape),
                                             ends[:, k:k + 1, :].to_broadcast(shape), ALU.is_ge))
                dve.tensor_reduce(t_expert[:, k, :], past[:, k], AX_X, ALU.add)
                table_next(dve.tensor_tensor(past_n[:, k], past[:, k], nt[:, None, :].to_broadcast(shape), ALU.mult))
                table_next(dve.tensor_reduce(t_start[:, k, :], past_n[:, k], AX_X, ALU.add))
                table_next(dve.scalar_tensor_tensor(t_row[:, k, :], t_expert[:, k, :], float(REG // P), it,
                                                    ALU.mult, ALU.add))
                table_next(dve.tensor_tensor(t_row[:, k, :], t_row[:, k, :], t_start[:, k, :], ALU.subtract))
                at = slice(k * TABLE, k * TABLE + EXPERT_TILES)
                dve.tensor_scalar(table_row[:, at], t_row[:, k, :], float(P), float(E * REG), ALU.mult, ALU.min)
                dve.tensor_scalar(table_expert[:, at], t_expert[:, k, :], float(E - 1), None, ALU.min)\
                    .then_inc(table_done, 1)

            def set_up_attention():
                dve.wait_ge(att_in, 16 * 6)
                dve.tensor_tensor(att_scale[:, 2:5], att_cols[:, 2:5], att_cols[:, 5:8], ALU.mult).then_inc(set_up, 1)
                dve.tensor_scalar(att_scale[:, 1:2], att_cols[:, 1:2], 8 * C1 ** 3, None, ALU.mult)\
                    .then_inc(set_up, 1)
                dve.wait_ge(set_up, 3)
                dve.scalar_tensor_tensor(att_scale[:, 0:1], att_cols[:, 0:1], 8 * C1 ** 3, att_scale[:, 2:3],
                                         ALU.mult, ALU.mult).then_inc(set_up, 1)

            moments_of(0)
            rstd_of(0)
            normalize(0)
            dve.wait_ge(const_in, 16)
            dve.tensor_copy(before[:, :], before_f[:, :])
            dve.tensor_copy(carry[:, :], region).then_inc(set_up, 1)
            moments_of(1)
            rstd_of(1)
            normalize(1)
            dve.wait_ge(gate_bias_in, 16)
            route(0)
            moments_of(2)
            weights(0)
            place_rows(0)
            moments_of(3)
            rstd_of(2)
            route(1)
            for g in range(2, GROUPS):
                normalize(g)
            weights(1)
            place_rows(1)
            set_up_attention()
            dve.wait_ge(b_in, 16)
            dve.tensor_copy(b2_part[:, 0, :], b2_row[:, :]).then_inc(b_parts, 1)
            dve.wait_ge(b_parts, 1)
            dve.tensor_tensor(b2_rest[:, 0, :], b2_row[:, :], b2_part[:, 0, :], ALU.subtract).then_inc(b_parts, 1)
            dve.wait_ge(b_parts, 2)
            dve.tensor_copy(b2_part[:, 1, :], b2_rest[:, 0, :]).then_inc(b_parts, 1)
            dve.wait_ge(b_parts, 3)
            dve.tensor_tensor(b2_rest[:, 1, :], b2_rest[:, 0, :], b2_part[:, 1, :], ALU.subtract).then_inc(b_parts, 1)
            dve.wait_ge(b_parts, 4)
            dve.tensor_copy(b2_part[:, 2, :], b2_rest[:, 1, :]).then_inc(b_parts, 1)
            for g in range(2, GROUPS):
                route(g)
                weights(g)
                place_rows(g)
            pad_places()
            attention(0)
            tile_counts()
            attention(1)
            tile_table(0)
            for n in range(2, BEFORE):
                attention(n)
            tile_table(1)

            ps = passes[0]

            def step1(t, turn, j, _=None, fresh=False):
                a, b = row_in[j], row_out[j]
                if not fresh:
                    dve.wait_ge(ps.sent[j], 16 * turn)
                dve.wait_ge(ps.o_psum, t + 1)
                dve.tensor_copy(place[j][:, :], a[:, P:P + 1])
                eo = ps_o[j % 2][:, 0:P]
                dve.scalar_tensor_tensor(b[:, 0:P], eo, 0.5, a[:, 0:P], ALU.mult, ALU.add)
                dve.scalar_tensor_tensor(b[:, P:2 * P], eo, a[:, P + 1:P + 2], a[:, 0:P], ALU.mult, ALU.add)\
                    .then_inc(ps.o_read, 1)
                dve.tensor_copy(b[:, 2 * P:2 * P + 2], a[:, P + 2:P + 4]).then_inc(ps.row_read, 1)

            for t in range(RING):
                step1(t, 0, t, fresh=True)
            tiles(dve, RING, EXPERT_TILES, step1)

            for n in range(BEFORE, BETWEEN):
                attention(n)

            ps2 = passes[1]

            def mix(t, j):
                c = j % 2
                dve.wait_ge(ps2.o_psum, t + 1)
                dve.scalar_tensor_tensor(res[c][:, :], ps_o[c][:, 0:P], row_in[j][:, 2 * P:2 * P + 1],
                                         row_in[j][:, P:2 * P], ALU.mult, ALU.add).then_inc(ps2.o_read, 1)

            def statistics(t, j):
                dve.wait_ge(ps2.o_read, t + 1)
                dve.bn_stats(st2[j % 2][:, :], res[j % 2][:, :]).then_inc(ps2.stats, 1)

            def spread(t, j):
                dve.bn_aggr(mv2[j % 2][:, :], st2[j % 2][:, :]).then_inc(ps2.moments, 1)

            def centre(t, j):
                dve.wait_ge(ps2.moments, t + 1)
                dve.scalar_tensor_tensor(cent[j % 4][:, :], res[j % 2][:, :], mv2[j % 2][:, 0:1], gamma_bc[:, :],
                                         ALU.subtract, ALU.mult).then_inc(ps2.cent, 1)

            def invert(t, j):
                dve.wait_ge(ps2.std, t + 1)
                dve.reciprocal(rstd2[j % 2][:, :], std2[j % 2][:, :]).then_inc(ps2.rstd, 1)

            def finish(t, j):
                dve.wait_ge(ps2.cent, t + 1)
                dve.wait_ge(ps2.rstd, t + 1)
                dve.scalar_tensor_tensor(row_out[j][:, 0:P], cent[j % 4][:, :], rstd2[j % 2][:, 0:1],
                                         beta_bc[:, :], ALU.mult, ALU.add).then_inc(ps2.row_done, 1)

            def token(t, turn, j, fresh):
                if fresh:
                    dve.wait_ge(passes[0].sent[j], 16 * len(range(j, EXPERT_TILES, RING)))
                else:
                    dve.wait_ge(ps2.sent[j], 16 * turn)
                dve.tensor_copy(place[j][:, :], row_in[j][:, 2 * P + 1:2 * P + 2]).then_inc(ps2.row_read, 1)

            def step2(t, turn, j, _=None, fresh=False, behind=2):
                j1, j2 = (j - 1) % RING, (j - 2) % RING
                mix(t, j)
                if behind > 1:
                    invert(t - 2, j2)
                if behind > 0:
                    centre(t - 1, j1)
                statistics(t, j)
                if behind > 1:
                    finish(t - 2, j2)
                dve.wait_ge(ps2.stats, t + 1)
                token(t, turn, j, fresh)
                spread(t, j)

            for t in range(RING):
                step2(t, 0, t, fresh=True, behind=min(t, 2))
            tiles(dve, RING, EXPERT_TILES, step2)
            t = EXPERT_TILES
            centre(t - 1, (t - 1) % RING)
            for n in (t - 2, t - 1):
                invert(n, n % RING)
                finish(n, n % RING)

            for what, n in tail_order():
                if what == "attention":
                    attention(n)
                elif n not in POOL_GATES:
                    gate_step(dve, n)



def kernel(L0_attn_query, L0_attn_W_qkv, L0_attn_b_qkv, L0_attn_W_out, L0_attn_b_out, L0_attn_weight_q,
           L0_attn_weight_v, L0_ffn_gate_W, L0_ffn_gate_b, L0_ffn_W1, L0_ffn_b1, L0_ffn_W2, L0_ffn_b2,
           L0_ffn_ln_gamma, L0_ffn_ln_beta):
    import concourse.bacc as bacc
    from concourse.bass_utils import run_bass_kernel_spmd

    a = np.asarray
    wqkv, bqkv = a(L0_attn_W_qkv), a(L0_attn_b_qkv)
    arrays = {
        "query": a(L0_attn_query),
        "wq_t": wqkv[0:P].T, "wv_t": wqkv[2 * P:3 * P].T, "wo_t": a(L0_attn_W_out).T,
        "att_cols": np.concatenate([bqkv[0:P, None], bqkv[2 * P:3 * P, None],
                                    a(L0_attn_weight_q).transpose(0, 2, 1).reshape(P, 3),
                                    a(L0_attn_weight_v).transpose(0, 2, 1).reshape(P, 3)], axis=1),
        "vectors": np.concatenate([a(L0_attn_b_out), a(L0_ffn_ln_gamma), a(L0_ffn_ln_beta)]),
        "gate_w": a(L0_ffn_gate_W), "gate_b": a(L0_ffn_gate_b),
        "w1": a(L0_ffn_W1), "w2": a(L0_ffn_W2),
        "b1": a(L0_ffn_b1).reshape(E, 2, P).transpose(2, 0, 1), "b2": a(L0_ffn_b2),
    }
    arrays.update(consts())
    arrays = {n: np.ascontiguousarray(v) for n, v in arrays.items()}
    nc = bacc.Bacc("TRN2", target_bir_lowering=False, num_devices=1)
    io = {n: nc.dram_tensor(f"in_{n}", v.shape, mybir.dt.from_np(v.dtype), kind="ExternalInput").ap()
          for n, v in arrays.items()}
    out = nc.dram_tensor("out", (16, 256, P), F32, kind="ExternalOutput").ap()
    build(nc, io, out)
    r = run_bass_kernel_spmd(nc, [{f"in_{n}": v for n, v in arrays.items()}], core_ids=[0])
    return r.results[0]["out"]
```
